# Optimizing a Trainium2 kernel written in Bass

```python
import numpy as np
import jax
import jax.numpy as jnp

def _softmax(x, axis=-1):
    return jax.nn.softmax(x, axis=axis)

def _gelu(x):
    return jax.nn.gelu(x, approximate=True)

def _silu(x):
    return jax.nn.silu(x)

def _sigmoid(x):
    return jax.nn.sigmoid(x)

def _layernorm(x, axis=-1, eps=1e-05):
    m = jnp.mean(x, axis=axis, keepdims=True)
    v = jnp.var(x, axis=axis, keepdims=True)
    return (x - m) / jnp.sqrt(v + eps)

def _scatter_add(tgt, idx, src, axis=0):
    return tgt.at[idx].add(src)

def _segment_sum(src, seg, n):
    return jax.ops.segment_sum(src, seg, n)
kernel_name = 'mk_vit_tower_d1_tok_img512_r4_31053d'

def setup_inputs(seed: int=0):
    np.random.seed(seed)
    _w = jnp.asarray

    def _rec_inputs():
        import jax
        import jax.numpy as jnp
        _rk = jax.random.key(seed)
        x = -0.000356955 + 1 * jax.random.normal(jax.random.fold_in(_rk, 1), (32, 3, 112, 112), jnp.float32)
        return x
    x = _rec_inputs()

    def _L0_tok_setup():
        import jax, jax.numpy as jnp
        import numpy as np
        IMG = 112
        P = 16
        C = 3
        D = 128
        DC = 8
        DS = 4
        NH = IMG // P
        NPATCH = NH * NH
        PDIM = C * P * P
        BATCH = 32
        EPS = 1e-05
        key = jax.random.key(seed)
        ks = jax.random.split(key, 10)

        def lin(k, fan_in, shape):
            bound = 1.0 / np.sqrt(fan_in)
            return jax.random.uniform(k, shape, jnp.float32, -bound, bound)
        return {'images': jax.random.normal(ks[0], (BATCH, C, IMG, IMG), jnp.float32), 'W_patch': lin(ks[1], PDIM, (PDIM, D)), 'b_patch': jnp.zeros((D,), jnp.float32), 'pos_embed': jax.random.normal(ks[2], (1, NPATCH, D), jnp.float32) * 0.02, 'W_coord': lin(ks[3], D, (D, DC)), 'b_coord': jnp.zeros((DC,), jnp.float32), 'W_spinor': lin(ks[4], D, (D, DS)), 'b_spinor': jnp.zeros((DS,), jnp.float32), 'W_embed': lin(ks[5], DC, (DC, D)), 'b_embed': jnp.zeros((D,), jnp.float32), 'ln_gamma': jnp.ones((D,), jnp.float32), 'ln_beta': jnp.zeros((D,), jnp.float32), 'W_out': lin(ks[6], D, (D, D)), 'b_out': jnp.zeros((D,), jnp.float32)}
    _L0_tok_all = _L0_tok_setup()
    _L0_tok_in = {k: v for k, v in _L0_tok_all.items() if k in ('W_patch', 'b_patch', 'pos_embed', 'W_coord', 'b_coord', 'W_spinor', 'b_spinor', 'W_embed', 'b_embed', 'ln_gamma', 'ln_beta', 'W_out', 'b_out')}
    del _L0_tok_all

    def _L0_attn_setup():
        import jax, jax.numpy as jnp
        import numpy as np
        D_MODEL = 128
        N_HEADS = 8
        HEAD_DIM = D_MODEL // N_HEADS
        WINDOW = 5

        def _ocr_pattern_mask(S, dtype):
            idx = jnp.arange(S)
            band = jnp.abs(idx[:, None] - idx[None, :]) <= WINDOW
            return jnp.where(band, jnp.asarray(0.1, dtype), jnp.asarray(0.0, dtype))
        key = jax.random.key(seed)
        ks = jax.random.split(key, 12)
        B, S = (4, 512)
        x = jax.random.normal(ks[0], (B, S, D_MODEL), dtype=jnp.float32)
        ocr_context = jax.random.randint(ks[1], (B, S), 0, 100, dtype=jnp.int64)
        scale = 0.02
        Wq = jax.random.normal(ks[2], (D_MODEL, D_MODEL), dtype=jnp.float32) * scale
        bq = jax.random.normal(ks[3], (D_MODEL,), dtype=jnp.float32) * scale
        Wk = jax.random.normal(ks[4], (D_MODEL, D_MODEL), dtype=jnp.float32) * scale
        bk = jax.random.normal(ks[5], (D_MODEL,), dtype=jnp.float32) * scale
        Wv = jax.random.normal(ks[6], (D_MODEL, D_MODEL), dtype=jnp.float32) * scale
        bv = jax.random.normal(ks[7], (D_MODEL,), dtype=jnp.float32) * scale
        Wo = jax.random.normal(ks[8], (D_MODEL, D_MODEL), dtype=jnp.float32) * scale
        bo = jax.random.normal(ks[9], (D_MODEL,), dtype=jnp.float32) * scale
        ocr_bias = jax.random.normal(ks[10], (D_MODEL,), dtype=jnp.float32)
        return {'x': x, 'ocr_context': ocr_context, 'Wq': Wq, 'bq': bq, 'Wk': Wk, 'bk': bk, 'Wv': Wv, 'bv': bv, 'Wo': Wo, 'bo': bo, 'ocr_bias': ocr_bias}
    _L0_attn_all = _L0_attn_setup()
    _L0_attn_in = {k: v for k, v in _L0_attn_all.items() if k in ('ocr_context', 'Wq', 'bq', 'Wk', 'bk', 'Wv', 'bv', 'Wo', 'bo', 'ocr_bias')}
    del _L0_attn_all

    def _L0_ffn_setup():
        import jax, jax.numpy as jnp
        import numpy as np
        TOP_K = 6
        CAP_FACTOR = 2.0
        key = jax.random.key(seed)
        ks = jax.random.split(key, 9)
        B, S, D, F, E, SH = (4, 512, 128, 64, 64, 2)
        return {'x': jax.random.normal(ks[0], (B, S, D), jnp.float32), 'router_w': jax.random.normal(ks[1], (E, D), jnp.float32) * 0.02, 'bias': jnp.zeros((E,), jnp.float32), 'shared_w_gate': jax.random.normal(ks[2], (SH, F, D), jnp.float32) * 0.02, 'shared_w_up': jax.random.normal(ks[3], (SH, F, D), jnp.float32) * 0.02, 'shared_w_down': jax.random.normal(ks[4], (SH, D, F), jnp.float32) * 0.02, 'w_gate': jax.random.normal(ks[5], (E, F, D), jnp.float32) * 0.02, 'w_up': jax.random.normal(ks[6], (E, F, D), jnp.float32) * 0.02, 'w_down': jax.random.normal(ks[7], (E, D, F), jnp.float32) * 0.02}
    _L0_ffn_all = _L0_ffn_setup()
    _L0_ffn_in = {k: v for k, v in _L0_ffn_all.items() if k in ('router_w', 'bias', 'shared_w_gate', 'shared_w_up', 'shared_w_down', 'w_gate', 'w_up', 'w_down')}
    del _L0_ffn_all
    return {'x': x, 'L0_tok_W_patch': _L0_tok_in['W_patch'], 'L0_tok_b_patch': _L0_tok_in['b_patch'], 'L0_tok_pos_embed': _L0_tok_in['pos_embed'], 'L0_tok_W_coord': _L0_tok_in['W_coord'], 'L0_tok_b_coord': _L0_tok_in['b_coord'], 'L0_tok_W_spinor': _L0_tok_in['W_spinor'], 'L0_tok_b_spinor': _L0_tok_in['b_spinor'], 'L0_tok_W_embed': _L0_tok_in['W_embed'], 'L0_tok_b_embed': _L0_tok_in['b_embed'], 'L0_tok_ln_gamma': _L0_tok_in['ln_gamma'], 'L0_tok_ln_beta': _L0_tok_in['ln_beta'], 'L0_tok_W_out': _L0_tok_in['W_out'], 'L0_tok_b_out': _L0_tok_in['b_out'], 'L0_attn_ocr_context': _L0_attn_in['ocr_context'], 'L0_attn_Wq': _L0_attn_in['Wq'], 'L0_attn_bq': _L0_attn_in['bq'], 'L0_attn_Wk': _L0_attn_in['Wk'], 'L0_attn_bk': _L0_attn_in['bk'], 'L0_attn_Wv': _L0_attn_in['Wv'], 'L0_attn_bv': _L0_attn_in['bv'], 'L0_attn_Wo': _L0_attn_in['Wo'], 'L0_attn_bo': _L0_attn_in['bo'], 'L0_attn_ocr_bias': _L0_attn_in['ocr_bias'], 'L0_ffn_router_w': _L0_ffn_in['router_w'], 'L0_ffn_bias': _L0_ffn_in['bias'], 'L0_ffn_shared_w_gate': _L0_ffn_in['shared_w_gate'], 'L0_ffn_shared_w_up': _L0_ffn_in['shared_w_up'], 'L0_ffn_shared_w_down': _L0_ffn_in['shared_w_down'], 'L0_ffn_w_gate': _L0_ffn_in['w_gate'], 'L0_ffn_w_up': _L0_ffn_in['w_up'], 'L0_ffn_w_down': _L0_ffn_in['w_down']}

def reference(x, L0_tok_W_patch, L0_tok_b_patch, L0_tok_pos_embed, L0_tok_W_coord, L0_tok_b_coord, L0_tok_W_spinor, L0_tok_b_spinor, L0_tok_W_embed, L0_tok_b_embed, L0_tok_ln_gamma, L0_tok_ln_beta, L0_tok_W_out, L0_tok_b_out, L0_attn_ocr_context, L0_attn_Wq, L0_attn_bq, L0_attn_Wk, L0_attn_bk, L0_attn_Wv, L0_attn_bv, L0_attn_Wo, L0_attn_bo, L0_attn_ocr_bias, L0_ffn_router_w, L0_ffn_bias, L0_ffn_shared_w_gate, L0_ffn_shared_w_up, L0_ffn_shared_w_down, L0_ffn_w_gate, L0_ffn_w_up, L0_ffn_w_down):
    import jax
    import jax.numpy as jnp

    def _L0_tok_ref(images, W_patch, b_patch, pos_embed, W_coord, b_coord, W_spinor, b_spinor, W_embed, b_embed, ln_gamma, ln_beta, W_out, b_out):
        import jax, jax.numpy as jnp
        import numpy as np
        IMG = 112
        P = 16
        C = 3
        D = 128
        DC = 8
        DS = 4
        NH = IMG // P
        NPATCH = NH * NH
        PDIM = C * P * P
        BATCH = 32
        EPS = 1e-05
        B = images.shape[0]
        patches = images.reshape(B, C, NH, P, NH, P)
        patches = patches.transpose(0, 2, 4, 1, 3, 5).reshape(B, NPATCH, PDIM)
        x = patches @ W_patch + b_patch + pos_embed
        coords = x @ W_coord + b_coord
        spinor = x @ W_spinor + b_spinor
        K0 = jnp.sum(spinor * spinor, axis=-1)
        x_manifold = coords @ W_embed + b_embed
        x_enh = x_manifold * K0[..., None] + x
        mu = jnp.mean(x_enh, axis=-1, keepdims=True)
        var = jnp.mean(jnp.square(x_enh - mu), axis=-1, keepdims=True)
        x_norm = (x_enh - mu) * jax.lax.rsqrt(var + EPS) * ln_gamma + ln_beta
        return x_norm @ W_out + b_out

    def _L0_attn_ref(x, ocr_context, Wq, bq, Wk, bk, Wv, bv, Wo, bo, ocr_bias):
        import jax, jax.numpy as jnp
        import numpy as np
        D_MODEL = 128
        N_HEADS = 8
        HEAD_DIM = D_MODEL // N_HEADS
        WINDOW = 5

        def _ocr_pattern_mask(S, dtype):
            idx = jnp.arange(S)
            band = jnp.abs(idx[:, None] - idx[None, :]) <= WINDOW
            return jnp.where(band, jnp.asarray(0.1, dtype), jnp.asarray(0.0, dtype))
        B, S, D = x.shape
        H, hd = (N_HEADS, HEAD_DIM)
        q = (x @ Wq.T + bq).reshape(B, S, H, hd)
        k = (x @ Wk.T + bk).reshape(B, S, H, hd)
        v = (x @ Wv.T + bv).reshape(B, S, H, hd)
        q = q + ocr_bias.reshape(H, hd)
        scores = jnp.einsum('bqhd,bkhd->bhqk', q, k) / np.sqrt(hd).astype(x.dtype)
        scores = scores + _ocr_pattern_mask(S, scores.dtype)
        attn = jax.nn.softmax(scores, axis=-1)
        out = jnp.einsum('bhqk,bkhd->bqhd', attn, v).reshape(B, S, D)
        return out @ Wo.T + bo

    def _L0_ffn_ref(x, router_w, bias, shared_w_gate, shared_w_up, shared_w_down, w_gate, w_up, w_down):
        import jax, jax.numpy as jnp
        import numpy as np
        TOP_K = 6
        CAP_FACTOR = 2.0
        B, S, D = x.shape
        E = router_w.shape[0]
        K = TOP_K
        N = B * S
        C = max(1, int(N * K * CAP_FACTOR / E))
        router_logits = jnp.einsum('bsd,ed->bse', x, router_w) + bias
        hg = jnp.einsum('bsd,efd->bsef', x, shared_w_gate)
        hu = jnp.einsum('bsd,efd->bsef', x, shared_w_up)
        shared_out = jnp.einsum('bsef,edf->bsd', jax.nn.silu(hg) * hu, shared_w_down)
        shared_out = shared_out / shared_w_gate.shape[0]
        router_probs = jax.nn.softmax(router_logits, axis=-1)
        topk_p, topk_i = jax.lax.top_k(router_probs, K)
        topk_p = topk_p / (jnp.sum(topk_p, axis=-1, keepdims=True) + 1e-09)
        x_flat = x.reshape(N, D)
        flat_e = topk_i.reshape(-1)
        flat_g = topk_p.reshape(-1)
        token_ids = jnp.repeat(jnp.arange(N), K)
        order = jnp.argsort(flat_e)
        se = flat_e[order]
        st = token_ids[order]
        sg = flat_g[order]
        M = se.shape[0]
        pos = jnp.arange(M)
        is_first = jnp.concatenate([jnp.ones((1,), bool), se[1:] != se[:-1]])
        group_starts = jax.lax.cummax(pos * is_first.astype(pos.dtype))
        slot = pos - group_starts
        valid = slot < C
        safe_slot = jnp.where(valid, slot, C)
        expert_in = jnp.zeros((E, C + 1, D), x.dtype).at[se, safe_slot].set(x_flat[st])
        expert_gate = jnp.zeros((E, C + 1), x.dtype).at[se, safe_slot].set(sg)
        expert_tok = jnp.full((E, C + 1), N, jnp.int32).at[se, safe_slot].set(st.astype(jnp.int32))
        expert_mask = jnp.zeros((E, C + 1), bool).at[se, safe_slot].set(valid)
        expert_in = expert_in[:, :C]
        expert_gate = expert_gate[:, :C]
        expert_tok = expert_tok[:, :C]
        expert_mask = expert_mask[:, :C]
        hg = jnp.einsum('ecd,efd->ecf', expert_in, w_gate)
        hu = jnp.einsum('ecd,efd->ecf', expert_in, w_up)
        expert_out = jnp.einsum('ecf,edf->ecd', jax.nn.silu(hg) * hu, w_down)
        fm = expert_mask.reshape(-1)
        dst = jnp.where(fm, expert_tok.reshape(-1), N)
        fg = jnp.where(fm, expert_gate.reshape(-1), jnp.zeros((), x.dtype))
        sparse = jax.ops.segment_sum(fg[:, None] * expert_out.reshape(-1, D), dst, num_segments=N + 1)[:N]
        return shared_out + sparse.reshape(B, S, D)
    h = _L0_tok_ref(x, L0_tok_W_patch, L0_tok_b_patch, L0_tok_pos_embed, L0_tok_W_coord, L0_tok_b_coord, L0_tok_W_spinor, L0_tok_b_spinor, L0_tok_W_embed, L0_tok_b_embed, L0_tok_ln_gamma, L0_tok_ln_beta, L0_tok_W_out, L0_tok_b_out)
    h = h + _L0_attn_ref(_layernorm(h, axis=-1), L0_attn_ocr_context, L0_attn_Wq, L0_attn_bq, L0_attn_Wk, L0_attn_bk, L0_attn_Wv, L0_attn_bv, L0_attn_Wo, L0_attn_bo, L0_attn_ocr_bias)
    h = h + _L0_ffn_ref(_layernorm(h, axis=-1), L0_ffn_router_w, L0_ffn_bias, L0_ffn_shared_w_gate, L0_ffn_shared_w_up, L0_ffn_shared_w_down, L0_ffn_w_gate, L0_ffn_w_up, L0_ffn_w_down)
    return h

_drawn_inputs = setup_inputs


def setup_inputs(seed=0):
    import zlib

    import numpy as np

    out = dict(_drawn_inputs(seed))
    spreads = {'L0_tok_b_patch': (0.0, 0.1),
     'L0_tok_b_coord': (0.0, 0.1),
     'L0_tok_b_spinor': (0.0, 0.1),
     'L0_tok_b_embed': (0.0, 0.1),
     'L0_tok_ln_gamma': (1.0, 0.2),
     'L0_tok_ln_beta': (0.0, 0.1),
     'L0_tok_b_out': (0.0, 0.1),
     'L0_ffn_bias': (0.0, 0.8)}
    factors = {'L0_attn_Wq': 8.0,
     'L0_attn_bq': 8.0,
     'L0_attn_Wk': 8.0,
     'L0_attn_bk': 8.0,
     'L0_attn_bv': 7.944,
     'L0_attn_ocr_bias': 8.0,
     'L0_ffn_router_w': 8.0,
     'L0_ffn_shared_w_gate': 8.0,
     'L0_ffn_shared_w_up': 8.0,
     'L0_ffn_shared_w_down': 8.0,
     'L0_ffn_w_gate': 8.0,
     'L0_ffn_w_up': 8.0,
     'L0_ffn_w_down': 8.0}
    for name, (base, spread) in spreads.items():
        noise = np.random.default_rng([zlib.crc32(name.encode()), seed]).standard_normal(out[name].shape)
        drawn = base * np.exp(spread * noise) if base else spread * noise
        out[name] = jnp.asarray(drawn.astype(out[name].dtype))
    for name, factor in factors.items():
        out[name] = (out[name] * factor).astype(out[name].dtype)
    return out
```

```python
from contextlib import ExitStack

import numpy as np

import concourse.bass as bass
from concourse import mybir

F32 = mybir.dt.float32
F32R = mybir.dt.float32r
ACT = mybir.ActivationFunctionType
ALU = mybir.AluOpType
AX_X = mybir.AxisListType.X

P = 128
IMAGES, CHANNELS, IMG, PATCH = 32, 3, 112, 16
GRID = IMG // PATCH
SEQ = GRID * GRID
N = IMAGES * SEQ
KT = CHANNELS * PATCH * PATCH // P
DC, DS = 8, 4
HEADS, HD = 8, 16
HP = HEADS // 2
WINDOW = 5
E, FF, TOPK, SHARED = 64, 64, 6, 2
CAPACITY = max(1, int(N * TOPK * 2.0 / E))
EPS = 1e-5

CH = 4
CI = IMAGES // CH
CW = CI * SEQ
PW = 2 * SEQ
PAIRS = IMAGES // 2
TILES = CW // PW
QW = 64
XP = E // 2
LAG = 2
WS = 4
SENTINEL = -3.0e38

W_COORD, W_SPIN, W_OUT, W_Q, W_K, W_V, W_O, W_ROUTER, W_EMBED = 0, 8, 12, 140, 268, 396, 524, 1036, 1100
V0 = 1228
(V_PATCH, V_EMBED, V_GAMMA, V_BETA, V_OUT, V_BQ, V_BK, V_OCR, V_BO, V_COORD, V_SPIN,
 V_ROUTER, V_BV) = range(V0, V0 + 13)
W_POS = V0 + 14
WCOLS = W_POS + SEQ
C_IDENT, C_CENTER, C_MEAN, C_ONES, C_BANDQ = 0, 128, 256, 384, 512
C_BANDK, C_PARITY, C_IMAGE, C_EPS = 640, 640 + CW, 642 + CW, 644 + CW
C_HP = C_EPS + 1
CCOLS = C_HP + HP


def build(nc, patches, w_patch, weights, consts, experts, gate_scratch, out):
    ctx = ExitStack()
    with ctx:
        def sb(name, shape, dt=F32):
            return ctx.enter_context(nc.sbuf_tensor(name, shape, dt))

        def sem(name):
            return ctx.enter_context(nc.semaphore(name))

        wpatch = sb("wpatch", [P, KT, P])
        wts = sb("wts", [P, WCOLS])
        cst = sb("cst", [P, CCOLS])
        pat = sb("pat", [P, KT, N])
        posb = sb("posb", [P, SEQ])
        x0 = sb("x0", [P, CH, CW])
        coords = sb("coords", [DC, CH, CW])
        spin2 = sb("spin2", [DS, CH, CW])
        xman = sb("xman", [P, CH, CW])
        xenh = sb("xenh", [P, CH, CW])
        sq = sb("sq", [P, CH, CW])
        xmk = sq
        sd = sb("sd", [P, CH, CW])
        rstd = sb("rstd", [P, CH, CW])
        ynorm = x0
        h1 = sb("h1", [P, N])
        xn = sb("xn", [P, N])
        btok = sb("btok", [P, 1])
        bproj = sb("bproj", [P, 1])
        bq1 = sb("bq1", [P, 1])
        qscale = sb("qscale", [P, 2])
        qbias = sb("qbias", [P, 2])
        bandq = sb("bandq", [PW, P], F32R)
        bandk = sb("bandk", [PW, CW], F32R)
        xpair = sb("xpair", [P, 2, PW])
        kpair = sb("kpair", [P, 2, PW])
        khead = sb("khead", [P, 2, 2, HP, SEQ])
        qdiag = sb("qdiag", [P, 2, 2, 2, QW])
        vdiag = sb("vdiag", [PW, 2, HP, 2, 2 * HD])
        smax = sb("smax", [P, 2, HEADS])
        sshift = sb("sshift", [P, 2, CW])
        probs = sb("probs", [P, 2, HP, 2, SEQ])
        ssum = sb("ssum", [P, 2, HEADS])
        rsum = sb("rsum", [P, 2, HEADS])
        probsT = sb("probsT", [PW, 2, HP * P])
        onorm = sb("onorm", [P, 2, 2 * HP * HD])
        oT = sb("oT", [P, 2, 2, QW])
        h2 = sb("h2", [P, N])
        x2 = x0
        x2h = sb("x2h", [P, CH, CW], F32R)
        x2l = sb("x2l", [P, CH, CW], F32R)
        logT = xenh[0:E, :, :]
        logits = sb("logits", [PW, CH, TILES, E + 2])
        top8 = sb("top8", [PW, CH, TILES, 8])
        top6 = sb("top6", [PW, CH, TILES, 8])
        marked = sb("marked", [PW, CH, TILES, E + 2])
        lshift = sb("lshift", [PW, CH, TILES, E])
        lexp = sb("lexp", [PW, CH, TILES, E])
        lsel = sb("lsel", [PW, CH, TILES, E])
        lsum = sb("lsum", [PW, CH, 4, TILES])
        gsel = sb("gsel", [PW, CH, TILES, 2 * E])
        gT = pat[0:E, 2, :].rearrange("p (a b) -> p a b", a=CH)
        selT = pat[0:E, 3, :].rearrange("p (a b) -> p a b", a=CH)
        rank = pat[0:E, 4, :].rearrange("p (a b) -> p a b", a=CH)
        ones_row = sb("ones_row", [E, CW])
        gateT = pat[0:E, 5, :].rearrange("p (a b) -> p a b", a=CH)
        wraw = sb("wraw", [P, WS, 3 * P])
        wh = sb("wh", [P, 2, 2 * P], F32R)
        wl = sb("wl", [P, 2, 2 * P], F32R)
        gbc = pat[:, 0:2, :]
        act_g = sb("act_g", [P, 2, CW])
        prod = sb("prod", [P, 2, CW])
        hid = sb("hid", [P, 2, CW])
        result = xman

        bank = [ctx.enter_context(nc.psum_tensor(f"bank{i}", [P, 512], F32)) for i in range(8)]
        bA, bB = bank[0:4], bank[4:8]
        b_qk, b_v, b_s, b_pT, b_o, b_oT, b_proj = bank[0], bank[1], bank[2:4], bank[4], bank[5], bank[6], bank[7]

        s_wpatch, s_weights, s_consts = sem("wpatch_in"), sem("weights_in"), sem("consts_in")
        s_pat = [sem(f"patches_in{c}") for c in range(CH)]
        posb_ready, biasmm_ready, bias_ready = sem("posb_ready"), sem("biasmm_ready"), sem("bias_ready")
        bq1_ready, qbias_ready, band_ready = sem("bq1_ready"), sem("qbias_ready"), sem("band_ready")
        pads_ready = sem("pads_ready")
        x0_mm, x0_ready = sem("x0_mm"), sem("x0_ready")
        cs_mm, coords_ready, spin_ready = sem("cs_mm"), sem("coords_ready"), sem("spin_ready")
        man_mm, xman_ready, xmk_ready, xenh_ready = sem("man_mm"), sem("xman_ready"), sem("xmk_ready"), sem("xenh_ready")
        cen_mm = [sem(f"cen_mm{n}") for n in range(3)]
        sq_ready = [sem(f"sq_ready{n}") for n in range(3)]
        var_mm = [sem(f"var_mm{n}") for n in range(3)]
        sd_ready = [sem(f"sd_ready{n}") for n in range(3)]
        rstd_ready = [sem(f"rstd_ready{n}") for n in range(3)]
        norm_ready = [sem(f"norm_ready{n}") for n in range(3)]
        h1_mm, h1_ready = sem("h1_mm"), sem("h1_ready")
        khead_ready = sem("khead_ready")
        xpair_ready, qk_mm, q_ready, v_mm, vdiag_ready = sem("xpair_ready"), sem("qk_mm"), sem("qk_ready"), sem("v_mm"), sem("vdiag_ready")
        scores_mm, smax_ready, sshift_ready, probs_ready, ssum_ready, rsum_ready = (
            sem("scores_mm"), sem("smax_ready"), sem("sshift_ready"), sem("probs_ready"), sem("ssum_ready"), sem("rsum_ready"))
        pT_mm, probsT_ready, o_mm, onorm_ready, oT_mm, oT_ready, proj_mm, h2_ready = (
            sem("pT_mm"), sem("probsT_ready"), sem("o_mm"), sem("onorm_ready"), sem("oT_mm"), sem("oT_ready"), sem("proj_mm"), sem("h2_ready"))
        x2h_ready, x2l_ready = sem("x2h_ready"), sem("x2l_ready")
        logT_mm, logT_ready, logits_mm, logits_ready = sem("logT_mm"), sem("logT_ready"), sem("logits_mm"), sem("logits_ready")
        sentinel_ready, top8_ready, top6_ready, marked_ready, lsel_ready, lshift_ready, lexp_ready = (
            sem("sentinel_ready"), sem("top8_ready"), sem("top6_ready"), sem("marked_ready"), sem("lsel_ready"), sem("lshift_ready"), sem("lexp_ready"))
        lsum_step = sem("lsum_step")
        gsel_ready, gT_mm, gT_ready, selT_ready, rank_ready, gateT_ready, gate_stored = (
            sem("gsel_ready"), sem("gT_mm"), sem("gT_ready"), sem("selT_ready"), sem("rank_ready"), sem("gateT_ready"), sem("gate_stored"))
        s_wraw = [sem(f"expert_in{s}") for s in range(WS)]
        s_gbc = [sem(f"gates_in{s}") for s in range(2)]
        wh_ready, wl_ready = sem("wh_ready"), sem("wl_ready")
        gu_mm, actg_ready, prod_ready, hid_ready, down_mm = sem("gu_mm"), sem("actg_ready"), sem("prod_ready"), sem("hid_ready"), sem("down_mm")
        result_ready, s_out = sem("result_ready"), sem("out_stored")

        def w(a, n, rows=P):
            return wts[0:rows, a:a + n]

        def c_(a, n, rows=P):
            return cst[0:rows, a:a + n]

        ident = c_(C_IDENT, P)
        chunk = [slice(c * CW, (c + 1) * CW) for c in range(CH)]

        def bcast(ap, axis, count):
            ap = ap.unsqueeze(axis)
            shape = list(ap.shape)
            shape[axis] = count
            return ap.to_broadcast(shape)

        block = ctx.enter_context(nc.Block())

        @block.sync
        def _(sp):
            sp.dma_start(wpatch[:, :, :], w_patch).then_inc(s_wpatch, 16)
            sp.dma_start(pat[:, :, chunk[0]], patches[:, :, chunk[0]]).then_inc(s_pat[0], 16)
            sp.dma_start(wts[:, :], weights).then_inc(s_weights, 16)
            sp.dma_start(cst[:, :], consts).then_inc(s_consts, 16)
            for c in range(1, CH):
                sp.dma_start(pat[:, :, chunk[c]], patches[:, :, chunk[c]]).then_inc(s_pat[c], 16)
            for s in range(WS):
                sp.dma_start(wraw[:, s, :], experts[s]).then_inc(s_wraw[s], 16)
            for c in range(CH):
                sp.wait_ge(gateT_ready, c + 1)
                sp.dma_start(gate_scratch[:, chunk[c]], gateT[:, c, :]).then_inc(gate_stored, 16)
            sp.wait_ge(gate_stored, 16 * CH)

            def load_gates(j, s):
                sp.dma_start(gbc[:, s, :], bcast(gate_scratch[bass.ds(2 * j, 2), :], 1, FF)).then_inc(s_gbc[s], 16)

            def refill_weights(p, s):
                sp.wait_ge(down_mm, CH * (p - WS + 1))
                sp.dma_start(wraw[:, s, :], experts[bass.ds(p, 1), :, :].rearrange("a p n -> p (a n)")).then_inc(s_wraw[s], 16)

            def refill_gates(j, s):
                sp.wait_ge(hid_ready, CH * j)
                load_gates(j, s)

            load_gates(0, 0)
            load_gates(1, 1)
            with sp.Fori(0, (XP - 4) // WS) as r:
                q = 2 + WS * r
                for u in range(WS):
                    refill_weights(q + u + 2, u)
                    refill_gates(q + u, u % 2)
            refill_weights(XP, 0)
            refill_gates(XP - 2, 0)
            refill_gates(XP - 1, 1)
            for c in range(CH):
                sp.wait_ge(result_ready, c + 1)
                sp.dma_start(out[:, chunk[c]], result[:, c, :]).then_inc(s_out, 16)
            sp.wait_ge(s_out, 16 * CH)

        @block.tensor
        def _(pe):
            pe.wait_ge(s_wpatch, 16)
            for c in range(CH):
                pe.wait_ge(s_pat[c], 16)
                for k in range(KT):
                    last = pe.matmul(bA[c][:, 0:CW], wpatch[:, k, :], pat[:, k, chunk[c]], start=(k == 0), stop=(k == KT - 1))
                last.then_inc(x0_mm, 1)
            pe.wait_ge(s_weights, 16)
            pe.wait_ge(s_consts, 16)
            pe.matmul(bB[0][:, 0:1], w(W_OUT, P), w(V_BETA, 1), start=True, stop=True)
            for t in range(2):
                last = pe.matmul(bB[0][:, 1:2], w(W_O + t * P, P), w(V_BV + t, 1), start=(t == 0), stop=(t == 1))
            last.then_inc(biasmm_ready, 1)
            for c in range(CH):
                pe.wait_ge(x0_ready, c + 1)
                if c == 0:
                    pe.wait_ge(bias_ready, 2)
                pe.matmul(bB[c][0:DC, 0:CW], w(W_COORD, DC), x0[:, c, :], start=True, stop=True)
                pe.matmul(bA[c][0:DS, 0:CW], w(W_SPIN, DS), x0[:, c, :], start=True, stop=True).then_inc(cs_mm, 1)
            for c in range(CH):
                pe.wait_ge(coords_ready, c + 1)
                pe.matmul(bB[c][:, 0:CW], w(W_EMBED, P, DC), coords[:, c, :], start=True, stop=True)
                pe.wait_ge(spin_ready, c + 1)
                pe.matmul(bA[c][:, 0:CW], c_(C_ONES, P, DS), spin2[:, c, :], start=True, stop=True).then_inc(man_mm, 1)

            def centre(n, src, free, free_at):
                for c in range(CH):
                    pe.wait_ge(free, free_at(c))
                    pe.matmul(bA[c][:, 0:CW], c_(C_CENTER, P), src(c), start=True, stop=True).then_inc(cen_mm[n], 1)

            def variance(n):
                for c in range(CH):
                    pe.wait_ge(sq_ready[n], c + 1)
                    pe.matmul(bB[c][:, 0:CW], c_(C_MEAN, P), sq[:, c, :], start=True, stop=True).then_inc(var_mm[n], 1)

            centre(0, lambda c: xenh[:, c, :], xenh_ready, lambda c: c + 1)
            variance(0)
            for c in range(CH):
                pe.wait_ge(norm_ready[0], c + 1)
                pe.matmul(bB[c][:, 0:CW], w(W_OUT, P), ynorm[:, c, :], start=True, stop=True).then_inc(h1_mm, 1)
            centre(1, lambda c: h1[:, chunk[c]], h1_ready, lambda c: c + 1)
            variance(1)

            def project(i, s, first):
                pe.wait_ge(xpair_ready, i + 1)
                if not first:
                    pe.wait_ge(q_ready, i)
                pe.matmul(b_qk[:, 0:PW], w(W_Q, P), xpair[:, s, :], start=True, stop=True)
                pe.matmul(b_qk[:, PW:2 * PW], w(W_K, P), xpair[:, s, :], start=True, stop=True).then_inc(qk_mm, 1)

            def project_v(i, s, first):
                if not first:
                    pe.wait_ge(vdiag_ready, i)
                pe.matmul(b_v[0:PW, 0:P], xpair[:, s, :], w(W_V, P), start=True, stop=True).then_inc(v_mm, 1)

            def scores(i, s, first):
                pe.wait_ge(khead_ready, i + 1)
                pe.wait_ge(q_ready, i + 1)
                if not first:
                    pe.wait_ge(sshift_ready, i - 1)
                pe.matmul(b_s[s][:, 0:CW], bandq[:, :], bandk[:, :], start=True, stop=False)
                for m in range(2):
                    last = pe.matmul(b_s[s][:, 0:CW].rearrange("p (h m k) -> p h m k", h=HP, m=2)[:, :, m, :],
                                     qdiag[:, s, m, :, :].rearrange("p a b -> p (a b)"), khead[:, s, m, :, :], start=False, stop=(m == 1))
                last.then_inc(scores_mm, 1)

            def transpose_probs(i, s, first):
                pe.wait_ge(probs_ready, i + 1)
                if not first:
                    pe.wait_ge(probsT_ready, i)
                for hp in range(HP):
                    last = pe.transpose(b_pT[0:PW, hp * P:(hp + 1) * P], probs[:, s, hp, :, :].rearrange("p a b -> p (a b)"), ident)
                last.then_inc(pT_mm, 1)

            def weigh_values(i, s, first):
                pe.wait_ge(probsT_ready, i + 1)
                pe.wait_ge(vdiag_ready, i + 1)
                if not first:
                    pe.wait_ge(onorm_ready, i)
                for hp in range(HP):
                    last = pe.matmul(b_o[:, hp * 64:(hp + 1) * 64], probsT[:, s, hp * P:(hp + 1) * P],
                                     vdiag[:, s, hp, :, :].rearrange("p a b -> p (a b)"), start=True, stop=True)
                last.then_inc(o_mm, 1)

            def transpose_out(i, s, first):
                pe.wait_ge(onorm_ready, i + 1)
                if not first:
                    pe.wait_ge(oT_ready, i)
                pe.transpose(b_oT[:, 0:P], onorm[:, s, :], ident).then_inc(oT_mm, 1)

            def project_out(i, s, first):
                pe.wait_ge(oT_ready, i + 1)
                if not first:
                    pe.wait_ge(h2_ready, i)
                for m in range(2):
                    for t in range(2):
                        last = pe.matmul(b_proj[:, m * SEQ:(m + 1) * SEQ], w(W_O + (2 * m + t) * P, P),
                                         oT[:, s, t, 0:SEQ], start=(t == 0), stop=(t == 1))
                last.then_inc(proj_mm, 1)

            pe.wait_ge(norm_ready[1], CH)
            pe.wait_ge(band_ready, 2)
            project(0, 0, True)
            scores(0, 0, True)
            project(1, 1, False)
            project_v(0, 0, True)
            scores(1, 1, True)

            def finish(i, s, first):
                weigh_values(i, s, first)
                transpose_out(i, s, first)
                project_out(i, s, first)

            for i in (2, 3):
                project(i, i % 2, False)
                transpose_probs(i - 2, i % 2, i == 2)
                project_v(i - 1, 1 - i % 2, False)
                scores(i, i % 2, False)
                finish(i - 2, i % 2, i == 2)
            with pe.Fori(0, (PAIRS - 4) // 2) as r:
                i = 4 + 2 * r
                for s in range(2):
                    project(i + s, s, False)
                    transpose_probs(i + s - 2, s, False)
                    project_v(i + s - 1, 1 - s, False)
                    scores(i + s, s, False)
                    finish(i + s - 2, s, False)
            transpose_probs(PAIRS - 2, 0, False)
            project_v(PAIRS - 1, 1, False)
            finish(PAIRS - 2, 0, False)
            transpose_probs(PAIRS - 1, 1, False)
            finish(PAIRS - 1, 1, False)

            centre(2, lambda c: h2[:, chunk[c]], h2_ready, lambda c: PAIRS)
            variance(2)
            for c in range(CH):
                pe.wait_ge(norm_ready[2], c + 1)
                pe.matmul(bA[c][0:E, 0:CW], w(W_ROUTER, E), x2[:, c, :], start=True, stop=True).then_inc(logT_mm, 1)
            for c in range(CH):
                pe.wait_ge(logT_ready, c + 1)
                for t in range(TILES):
                    last = pe.transpose(bB[c][0:PW, t * E:(t + 1) * E], logT[:, c, t * PW:(t + 1) * PW], c_(C_IDENT, E, E))
                last.then_inc(logits_mm, 1)
            for c in range(CH):
                pe.wait_ge(gsel_ready, c + 1)
                for t in range(TILES):
                    last = pe.transpose(bA[c][:, t * PW:(t + 1) * PW], gsel[:, c, t, :], c_(C_IDENT, PW, PW))
                last.then_inc(gT_mm, 1)

            def gate_up(k, p, c, hs):
                g, u = bB[2 * (c % 2)], bB[2 * (c % 2) + 1]
                if c == 0:
                    pe.wait_ge(wl_ready, p + 1)
                pe.wait_ge(prod_ready, k - 1)
                for b, a in ((g, 0), (u, P)):
                    pe.matmul(b[:, 0:CW], wh[:, hs, a:a + P], x2h[:, c, :], start=True, stop=False)
                    pe.matmul(b[:, 0:CW], wh[:, hs, a:a + P], x2l[:, c, :], start=False, stop=False)
                    last = pe.matmul(b[:, 0:CW], wl[:, hs, a:a + P], x2h[:, c, :], start=False, stop=True)
                last.then_inc(gu_mm, 1)

            def down(k, c, slot):
                pe.wait_ge(hid_ready, k + 1)
                pe.matmul(bA[c][:, 0:CW], wraw[:, slot, 2 * P:3 * P], hid[:, c % 2, :], start=False, stop=True,
                          skip_group_check=True).then_inc(down_mm, 1)

            pe.wait_ge(x2l_ready, CH)
            pe.wait_ge(logits_ready, CH)
            for c in range(CH):
                if c == 0:
                    pe.wait_ge(wl_ready, 1)
                if c < LAG:
                    g, u = bB[2 * (c % 2)], bB[2 * (c % 2) + 1]
                    for b, a in ((g, 0), (u, P)):
                        pe.matmul(b[:, 0:CW], wh[:, 0, a:a + P], x2h[:, c, :], start=True, stop=False)
                        pe.matmul(b[:, 0:CW], wh[:, 0, a:a + P], x2l[:, c, :], start=False, stop=False)
                        last = pe.matmul(b[:, 0:CW], wl[:, 0, a:a + P], x2h[:, c, :], start=False, stop=True)
                    last.then_inc(gu_mm, 1)
                else:
                    gate_up(c, 0, c, 0)
                    if c == LAG:
                        pe.wait_ge(selT_ready, CH)
                        for a in range(CH):
                            pe.matmul(bA[a][:, 0:CW], ident, h2[:, chunk[a]], start=True, stop=True)
                    down(c - LAG, c - LAG, 0)
            with pe.Fori(0, XP // WS) as r:
                j = WS * r
                for v in range(WS):
                    for c in range(CH):
                        gate_up(CH * (j + v + 1) + c, j + v + 1, c, (v + 1) % 2)
                        back = c - LAG
                        slot = (v + 1) % WS if back >= 0 else v
                        down(CH * (j + v + 1) + back, back % CH, slot)
            for c in range(LAG, CH):
                down(CH * XP + c, c, XP % WS)

        @block.scalar
        def _(act):
            act.wait_ge(s_weights, 16)
            act.wait_ge(s_consts, 16)
            for c in range(CH):
                act.wait_ge(cs_mm, c + 1)
                act.activation(coords[:, c, :], bB[c][0:DC, 0:CW], ACT.Identity, bias=w(V_COORD, 1, DC)).then_inc(coords_ready, 1)
                act.activation(spin2[:, c, :], bA[c][0:DS, 0:CW], ACT.Square, bias=w(V_SPIN, 1, DS)).then_inc(spin_ready, 1)
            for c in range(CH):
                act.wait_ge(man_mm, c + 1)
                act.activation(xman[:, c, :], bB[c][:, 0:CW], ACT.Identity, bias=w(V_EMBED, 1)).then_inc(xman_ready, 1)

            def spread(n):
                for c in range(CH):
                    act.wait_ge(cen_mm[n], c + 1)
                    act.activation(sq[:, c, :], bA[c][:, 0:CW], ACT.Square).then_inc(sq_ready[n], 1)
                for c in range(CH):
                    act.wait_ge(var_mm[n], c + 1)
                    act.activation(sd[:, c, :], bB[c][:, 0:CW], ACT.Sqrt, bias=c_(C_EPS, 1)).then_inc(sd_ready[n], 1)

            spread(0)
            act.wait_ge(bias_ready, 2)
            for c in range(CH):
                act.wait_ge(h1_mm, c + 1)
                act.activation(h1[:, chunk[c]], bB[c][:, 0:CW], ACT.Identity, bias=btok[:, :]).then_inc(h1_ready, 1)
            spread(1)

            def take_qk(i, s, first):
                act.wait_ge(qk_mm, i + 1)
                if not first:
                    act.wait_ge(scores_mm, i - 1)
                    act.wait_ge(khead_ready, i - 1)
                q = b_qk[:, 0:PW].rearrange("p (a b) -> p a b", a=2)
                for t in range(2):
                    act.activation(qdiag[:, s, :, t, 0:SEQ], q, ACT.Identity, bias=qbias[:, t:t + 1], scale=qscale[:, t:t + 1])
                act.activation(kpair[:, s, :], b_qk[:, PW:2 * PW], ACT.Identity, bias=w(V_BK, 1)).then_inc(q_ready, 1)

            def exponentials(i, s, first):
                act.wait_ge(sshift_ready, i + 1)
                if not first:
                    act.wait_ge(pT_mm, i - 1)
                act.activation(probs[:, s, :, :, :].rearrange("p a b c -> p (a b c)"), sshift[:, s, :], ACT.Exp).then_inc(probs_ready, 1)

            def take_probsT(i, s, first):
                act.wait_ge(pT_mm, i + 1)
                if not first:
                    act.wait_ge(o_mm, i - 1)
                act.activation(probsT[:, s, :], b_pT[0:PW, :], ACT.Identity).then_inc(probsT_ready, 1)

            def take_oT(i, s, first):
                act.wait_ge(oT_mm, i + 1)
                if not first:
                    act.wait_ge(proj_mm, i - 1)
                act.activation(oT[:, s, :, :].rearrange("p a b -> p (a b)"), b_oT[:, 0:P], ACT.Identity).then_inc(oT_ready, 1)

            act.wait_ge(pads_ready, 1)
            act.wait_ge(qbias_ready, 2)
            take_qk(0, 0, True)
            take_qk(1, 1, True)
            exponentials(0, 0, True)
            take_qk(2, 0, False)
            take_probsT(0, 0, True)
            exponentials(1, 1, True)
            take_oT(0, 0, True)
            take_qk(3, 1, False)
            take_probsT(1, 1, True)
            exponentials(2, 0, False)
            take_oT(1, 1, True)
            with act.Fori(0, (PAIRS - 4) // 2) as r:
                i = 4 + 2 * r
                for s in range(2):
                    take_qk(i + s, s, False)
                    take_probsT(i + s - 2, s, False)
                    exponentials(i + s - 1, 1 - s, False)
                    take_oT(i + s - 2, s, False)
            take_probsT(PAIRS - 2, 0, False)
            exponentials(PAIRS - 1, 1, False)
            take_oT(PAIRS - 2, 0, False)
            take_probsT(PAIRS - 1, 1, False)
            take_oT(PAIRS - 1, 1, False)

            def split_high(p, slot, hs, arrived, first=False):
                act.wait_ge(s_wraw[slot], arrived)
                if not first:
                    act.wait_ge(gu_mm, CH * (p - 1))
                act.activation(wh[:, hs, :], wraw[:, slot, 0:2 * P], ACT.Copy).then_inc(wh_ready, 1)

            split_high(0, 0, 0, 16, True)
            split_high(1, 1, 1, 16, True)

            spread(2)
            for c in range(CH):
                act.wait_ge(norm_ready[2], c + 1)
                act.activation(x2h[:, c, :], x2[:, c, :], ACT.Copy).then_inc(x2h_ready, 1)
                act.wait_ge(logT_mm, c + 1)
                act.activation(logT[:, c, :], bA[c][0:E, 0:CW], ACT.Identity, bias=w(V_ROUTER, 1, E)).then_inc(logT_ready, 1)
            for c in range(CH):
                act.wait_ge(lshift_ready, c + 1)
                act.activation(lexp[:, c, :, :], lshift[:, c, :, :], ACT.Exp).then_inc(lexp_ready, 1)

            def silu(k, c, first=False):
                act.wait_ge(gu_mm, k + 1)
                if not first:
                    act.wait_ge(prod_ready, k - 1)
                act.activation(act_g[:, c % 2, :], bB[2 * (c % 2)][:, 0:CW], ACT.Silu).then_inc(actg_ready, 1)

            for c in range(CH):
                silu(c, c, c < 2)
            with act.Fori(0, XP // WS - 1) as r:
                j = WS * r
                for v in range(WS):
                    for c in range(CH):
                        silu(CH * (j + v + 1) + c, c)
                        if c == 1:
                            split_high(j + v + 2, (v + 2) % WS, v % 2, 4 * j + (16 if v < 2 else 32))
            j = XP - WS
            for v in range(WS):
                for c in range(CH):
                    silu(CH * (j + v + 1) + c, c)
                    if c == 1 and j + v + 2 <= XP:
                        split_high(j + v + 2, (v + 2) % WS, v % 2, 4 * j + (16 if v < 2 else 32))

        @block.vector
        def _(dve):
            dve.wait_ge(s_weights, 16)
            dve.tensor_scalar(posb[:, :], w(W_POS, SEQ), w(V_PATCH, 1), None, ALU.add).then_inc(posb_ready, 1)
            dve.tensor_tensor(bq1[:, :], w(V_BQ, 1), w(V_OCR, 1), ALU.add).then_inc(bq1_ready, 1)
            dve.wait_ge(s_consts, 16)
            dve.tensor_scalar(qscale[:, :], c_(C_PARITY, 2), 1.0 / HD ** 0.5, None, ALU.mult).then_inc(qbias_ready, 1)
            dve.tensor_copy(bandq[:, :], c_(C_BANDQ, P, PW)).then_inc(band_ready, 1)
            dve.tensor_copy(bandk[:, :], c_(C_BANDK, CW, PW)).then_inc(band_ready, 1)
            dve.wait_ge(bq1_ready, 1)
            dve.wait_ge(qbias_ready, 1)
            dve.tensor_scalar(qbias[:, :], qscale[:, :], bq1[:, :], None, ALU.mult).then_inc(qbias_ready, 1)
            dve.wait_ge(posb_ready, 1)
            for c in range(CH):
                dve.wait_ge(x0_mm, c + 1)
                dve.tensor_tensor(x0[:, c, :].rearrange("p (a b) -> p a b", a=CI), bA[c][:, 0:CW].rearrange("p (a b) -> p a b", a=CI),
                                  bcast(posb[:, :], 1, CI), ALU.add).then_inc(x0_ready, 1)
            dve.wait_ge(biasmm_ready, 1)
            dve.tensor_tensor(btok[:, :], bB[0][:, 0:1], w(V_OUT, 1), ALU.add).then_inc(bias_ready, 1)
            dve.tensor_tensor(bproj[:, :], bB[0][:, 1:2], w(V_BO, 1), ALU.add).then_inc(bias_ready, 1)
            for c in range(CH):
                dve.wait_ge(xman_ready, c + 1)
                dve.tensor_tensor(xmk[:, c, :], bA[c][:, 0:CW], xman[:, c, :], ALU.mult).then_inc(xmk_ready, 1)
                dve.wait_ge(xmk_ready, c + 1)
                dve.tensor_tensor(xenh[:, c, :], xmk[:, c, :], x0[:, c, :], ALU.add).then_inc(xenh_ready, 1)

            def normalise(n, c):
                dve.wait_ge(sd_ready[n], c + 1)
                dve.reciprocal(rstd[:, c, :], sd[:, c, :]).then_inc(rstd_ready[n], 1)
                dve.wait_ge(rstd_ready[n], c + 1)

            for c in range(CH):
                normalise(0, c)
                dve.scalar_tensor_tensor(ynorm[:, c, :], bA[c][:, 0:CW], w(V_GAMMA, 1), rstd[:, c, :], ALU.mult, ALU.mult).then_inc(norm_ready[0], 1)
            for c in range(CH):
                normalise(1, c)
                dve.tensor_tensor(xn[:, chunk[c]], bA[c][:, 0:CW], rstd[:, c, :], ALU.mult).then_inc(norm_ready[1], 1)

            def shift(i, s, first):
                dve.wait_ge(scores_mm, i + 1)
                sc = b_s[s][:, 0:CW].rearrange("p (a b) -> p a b", a=HEADS)
                dve.tensor_reduce(smax[:, s, :], sc, AX_X, ALU.max).then_inc(smax_ready, 1)
                dve.wait_ge(smax_ready, i + 1)
                if not first:
                    dve.wait_ge(probs_ready, i - 1)
                dve.tensor_tensor(sshift[:, s, :].rearrange("p (a b) -> p a b", a=HEADS), sc, bcast(smax[:, s, :], 2, SEQ),
                                  ALU.subtract).then_inc(sshift_ready, 1)

            def take_v(i, s, first):
                dve.wait_ge(v_mm, i + 1)
                if not first:
                    dve.wait_ge(o_mm, i - 1)
                v = b_v[0:PW, 0:P].rearrange("p (a b) -> p a b", a=HP)
                dve.tensor_tensor(vdiag[:, s, :, :, :], bcast(v, 2, 2), bcast(bcast(c_(C_IMAGE, 2, PW), 1, HP), 3, 2 * HD),
                                  ALU.mult).then_inc(vdiag_ready, 1)

            def sums(i, s):
                dve.wait_ge(probs_ready, i + 1)
                dve.tensor_reduce(ssum[:, s, :], probs[:, s, :, :, :].rearrange("p a b c -> p (a b) c"), AX_X, ALU.add).then_inc(ssum_ready, 1)
                dve.wait_ge(ssum_ready, i + 1)
                dve.reciprocal(rsum[:, s, :], ssum[:, s, :]).then_inc(rsum_ready, 1)

            def take_o(i, s, first):
                dve.wait_ge(o_mm, i + 1)
                dve.wait_ge(rsum_ready, i + 1)
                if not first:
                    dve.wait_ge(oT_mm, i - 1)
                for t in range(2):
                    rows = slice(QW * t, QW * (t + 1))
                    o = b_o[rows, 0:4 * HP * HD].rearrange("p (h m t d) -> p h m t d", h=HP, m=2, t=2)[:, :, :, t, :]
                    r = rsum[rows, s, :].rearrange("p (h m) -> p h m", m=2)
                    last = dve.tensor_tensor(onorm[rows, s, :].rearrange("p (m h d) -> p h m d", m=2, h=HP), o, bcast(r, 3, HD), ALU.mult)
                last.then_inc(onorm_ready, 1)

            def residual(i):
                dve.wait_ge(proj_mm, i + 1)
                at = bass.ds(i * PW, PW)
                dve.scalar_tensor_tensor(h2[:, at], b_proj[:, 0:PW], bproj[:, :], h1[:, at], ALU.add, ALU.add).then_inc(h2_ready, 1)

            shift(0, 0, True)
            take_v(0, 0, True)
            sums(0, 0)
            shift(1, 1, True)
            take_v(1, 1, True)
            sums(1, 1)
            take_o(0, 0, True)
            residual(0)
            shift(2, 0, False)
            take_v(2, 0, False)
            sums(2, 0)
            take_o(1, 1, True)
            residual(1)
            with dve.Fori(0, (PAIRS - 1 - 3) // 2) as r:
                i = 3 + 2 * r
                for s in range(2):
                    shift(i + s, 1 - s, False)
                    take_v(i + s, 1 - s, False)
                    sums(i + s, 1 - s)
                    take_o(i + s - 1, s, False)
                    residual(i + s - 1)
            shift(PAIRS - 1, 1, False)
            take_v(PAIRS - 1, 1, False)
            sums(PAIRS - 1, 1)
            for j in (PAIRS - 2, PAIRS - 1):
                take_o(j, j % 2, False)
                residual(j)

            for c in range(CH):
                normalise(2, c)
                dve.tensor_tensor(x2[:, c, :], bA[c][:, 0:CW], rstd[:, c, :], ALU.mult).then_inc(norm_ready[2], 1)
            dve.wait_ge(pads_ready, 4)
            for c in range(CH):
                dve.wait_ge(logits_mm, c + 1)
                dve.tensor_copy(logits[:, c, :, 0:E], bB[c][0:PW, 0:TILES * E].rearrange("p (a b) -> p a b", a=TILES)).then_inc(logits_ready, 1)
            for c in range(CH):
                dve.wait_ge(logits_ready, c + 1)
                for t in range(TILES):
                    last = dve.max(top8[:, c, t, :], logits[:, c, t, 0:E])
                last.then_inc(top8_ready, 1)
                dve.wait_ge(top8_ready, c + 1)
                dve.tensor_tensor(lshift[:, c, :, :], logits[:, c, :, 0:E], bcast(top8[:, c, :, 0], 2, E), ALU.subtract).then_inc(lshift_ready, 1)
                dve.tensor_copy(top6[:, c, :, 0:TOPK], top8[:, c, :, 0:TOPK]).then_inc(top6_ready, 1)
                dve.wait_ge(top6_ready, c + 1)
                for t in range(TILES):
                    last = dve.match_replace(marked[:, c, t, :], top6[:, c, t, :], logits[:, c, t, :], -1.0e38)
                last.then_inc(marked_ready, 1)
                dve.wait_ge(marked_ready, c + 1)
                dve.tensor_tensor(gsel[:, c, :, E:2 * E], logits[:, c, :, 0:E], marked[:, c, :, 0:E], ALU.not_equal).then_inc(lsel_ready, 1)
            for c in range(CH):
                dve.wait_ge(lexp_ready, c + 1)
                dve.tensor_reduce(lsum[:, c, 0, :], lexp[:, c, :, :], AX_X, ALU.add).then_inc(lsum_step, 1)
                dve.wait_ge(lsel_ready, c + 1)
                dve.tensor_tensor(lsel[:, c, :, :], lexp[:, c, :, :], gsel[:, c, :, E:2 * E], ALU.mult).then_inc(lsum_step, 1)
                dve.wait_ge(lsum_step, 5 * c + 2)
                dve.tensor_reduce(lsum[:, c, 1, :], lsel[:, c, :, :], AX_X, ALU.add).then_inc(lsum_step, 1)
                dve.wait_ge(lsum_step, 5 * c + 3)
                dve.scalar_tensor_tensor(lsum[:, c, 2, :], lsum[:, c, 0, :], 1e-9, lsum[:, c, 1, :], ALU.mult, ALU.add).then_inc(lsum_step, 1)
                dve.wait_ge(lsum_step, 5 * c + 4)
                dve.reciprocal(lsum[:, c, 3, :], lsum[:, c, 2, :]).then_inc(lsum_step, 1)
                dve.wait_ge(lsum_step, 5 * c + 5)
                dve.tensor_tensor(gsel[:, c, :, 0:E], lsel[:, c, :, :], bcast(lsum[:, c, 3, :], 2, E), ALU.mult).then_inc(gsel_ready, 1)
            for c in range(CH):
                dve.wait_ge(gT_mm, c + 1)
                dve.tensor_copy(gT[:, c, :], bA[c][0:E, 0:CW]).then_inc(gT_ready, 1)
                dve.tensor_copy(selT[:, c, :], bA[c][E:2 * E, 0:CW]).then_inc(selT_ready, 1)
                dve.wait_ge(selT_ready, c + 1)
                if c:
                    dve.wait_ge(rank_ready, c)
                dve.tensor_tensor_scan(rank[:, c, :], ones_row[:, :], selT[:, c, :], rank[:, c - 1, CW - 1:CW] if c else 0.0,
                                       ALU.mult, ALU.add).then_inc(rank_ready, 1)
                dve.wait_ge(rank_ready, c + 1)
                dve.wait_ge(gT_ready, c + 1)
                dve.scalar_tensor_tensor(gateT[:, c, :], rank[:, c, :], float(CAPACITY), gT[:, c, :], ALU.is_le, ALU.mult).then_inc(gateT_ready, 1)

            def times_up(k, c, first=False):
                dve.wait_ge(actg_ready, k + 1)
                if not first:
                    dve.wait_ge(hid_ready, k - 1)
                dve.tensor_tensor(prod[:, c % 2, :], bB[2 * (c % 2) + 1][:, 0:CW], act_g[:, c % 2, :], ALU.mult).then_inc(prod_ready, 1)

            for c in range(CH):
                times_up(c, c, c < 2)
            with dve.Fori(0, XP // WS) as r:
                p = 1 + WS * r
                for v in range(WS):
                    for c in range(CH):
                        times_up(CH * (p + v) + c, c)
            for c in range(CH):
                dve.wait_ge(down_mm, CH * XP + c + 1)
                dve.tensor_copy(result[:, c, :], bA[c][:, 0:CW]).then_inc(result_ready, 1)

        @block.gpsimd
        def _(pool):
            pool.memset(qdiag[:, :, :, :, :], 0.0).then_inc(pads_ready, 1)
            pool.memset(logits[:, :, :, E:E + 2], SENTINEL).then_inc(pads_ready, 1)
            pool.memset(top6[:, :, :, TOPK:8], SENTINEL).then_inc(pads_ready, 1)
            pool.memset(ones_row[:, :], 1.0).then_inc(pads_ready, 1)

            def fetch_pair(i, s, first):
                if not first:
                    pool.wait_ge(v_mm, i - 1)
                    pool.wait_ge(qk_mm, i - 1)
                    pool.wait_ge(norm_ready[1], CH)
                pool.tensor_copy(xpair[:, s, :], xn[:, bass.ds(i * PW, PW)]).then_inc(xpair_ready, 1)

            def mask_k(i, s, first):
                pool.wait_ge(q_ready, i + 1)
                if not first:
                    pool.wait_ge(scores_mm, i - 1)
                pool.tensor_tensor(khead[:, s, :, :, :], bcast(kpair[:, s, :].rearrange("p (a b) -> p a b", a=2), 2, HP),
                                   bcast(bcast(c_(C_HP, HP), 1, 2), 3, SEQ), ALU.mult).then_inc(khead_ready, 1)

            pool.wait_ge(s_consts, 16)
            pool.wait_ge(norm_ready[1], CH)
            fetch_pair(0, 0, True)
            fetch_pair(1, 1, True)
            mask_k(0, 0, True)
            mask_k(1, 1, True)
            with pool.Fori(0, (PAIRS - 2) // 2) as r:
                i = 2 + 2 * r
                for s in range(2):
                    fetch_pair(i + s, s, False)
                    mask_k(i + s, s, False)

            def split_low(p, slot, hs, first=False):
                pool.wait_ge(wh_ready, p + 1)
                if not first:
                    pool.wait_ge(gu_mm, CH * (p - 1))
                pool.tensor_tensor(wl[:, hs, :], wraw[:, slot, 0:2 * P], wh[:, hs, :].bitcast(F32), ALU.subtract).then_inc(wl_ready, 1)

            split_low(0, 0, 0, True)
            for c in range(CH):
                pool.wait_ge(x2h_ready, c + 1)
                pool.tensor_tensor(x2l[:, c, :], x2[:, c, :], x2h[:, c, :].bitcast(F32), ALU.subtract).then_inc(x2l_ready, 1)
            split_low(1, 1, 1, True)
            for k in range(CH):
                pool.wait_ge(prod_ready, k + 1)
                if k >= 2:
                    pool.wait_ge(down_mm, k - 1)
                pool.tensor_scalar(hid[:, k % 2, :], prod[:, k % 2, :], 1.0 / SHARED, None, ALU.mult).then_inc(hid_ready, 1)

            def gated(k, c, gs):
                pool.wait_ge(prod_ready, k + 1)
                pool.wait_ge(down_mm, k - 1)
                pool.tensor_tensor(hid[:, c % 2, :], prod[:, c % 2, :], gbc[:, gs, chunk[c]], ALU.mult).then_inc(hid_ready, 1)

            with pool.Fori(0, (XP - WS) // WS) as r:
                j = WS * r
                for v in range(WS):
                    pool.wait_ge(s_gbc[v % 2], 8 * (j + v - v % 2) + 16)
                    for c in range(CH):
                        gated(CH * (j + v + 1) + c, c, v % 2)
                        if c == 1:
                            split_low(j + v + 2, (v + 2) % WS, v % 2)
            j = XP - WS
            for v in range(WS):
                pool.wait_ge(s_gbc[v % 2], 8 * (j + v - v % 2) + 16)
                for c in range(CH):
                    gated(CH * (j + v + 1) + c, c, v % 2)
                    if c == 1 and j + v + 2 <= XP:
                        split_low(j + v + 2, (v + 2) % WS, v % 2)


def _constants():
    c = np.zeros((P, CCOLS), np.float32)
    c[:, C_IDENT:C_IDENT + P] = np.eye(P)
    c[:, C_CENTER:C_CENTER + P] = np.eye(P) - 1.0 / P
    c[:, C_MEAN:C_MEAN + P] = 1.0 / P
    c[:, C_ONES:C_ONES + P] = 1.0
    tenth = np.float32(0.1)
    high = np.float32(np.round(float(tenth) * 2 ** 15) / 2 ** 15)
    eye = np.eye(SEQ, dtype=np.float32)
    idx = np.arange(SEQ)
    band = (np.abs(idx[:, None] - idx[None, :]) <= WINDOW).astype(np.float32)
    for r, part in enumerate((high, tenth - high)):
        for t in range(2):
            c[r * SEQ:(r + 1) * SEQ, C_BANDQ + t * QW:C_BANDQ + t * QW + SEQ] = eye * part
        c[r * SEQ:(r + 1) * SEQ, C_BANDK:C_BANDK + CW] = np.tile(band, (1, HEADS))
    for t in range(2):
        c[:, C_PARITY + t] = (np.arange(P) // HD) % 2 == t
        c[t * SEQ:(t + 1) * SEQ, C_IMAGE + t] = 1.0
    c[:, C_EPS] = EPS
    for hp in range(HP):
        c[:, C_HP + hp] = np.arange(P) // (2 * HD) == hp
    return c


def _rows(a):
    a = np.asarray(a)
    a = a.reshape(a.shape[0], -1)
    return np.concatenate([a, np.zeros((P - a.shape[0], a.shape[1]), a.dtype)]) if a.shape[0] < P else a


def kernel(**inputs):
    import concourse.bacc as _bacc
    from concourse.bass_utils import run_bass_kernel_spmd as _run

    f = {k: np.asarray(v) for k, v in inputs.items()}
    patches = f["x"].reshape(IMAGES, CHANNELS, GRID, PATCH, GRID, PATCH).transpose(1, 3, 5, 0, 2, 4).reshape(KT, P, N).transpose(1, 0, 2)
    w_patch = f["L0_tok_W_patch"].reshape(KT, P, P).transpose(1, 0, 2)
    wo = f["L0_attn_Wo"].T.reshape(HP, 2, HD, P).transpose(0, 2, 1, 3).reshape(HP * HD, 2 * P)
    blank = np.zeros_like(wo)
    wo = np.concatenate([np.concatenate([wo, blank], axis=1), np.concatenate([blank, wo], axis=1)])
    bv = f["L0_attn_bv"].reshape(HP, 2, HD).transpose(0, 2, 1).reshape(HP * HD, 2)
    columns = [f["L0_tok_W_coord"], f["L0_tok_W_spinor"], f["L0_tok_W_out"], f["L0_attn_Wq"].T, f["L0_attn_Wk"].T, f["L0_attn_Wv"].T,
               wo, f["L0_ffn_router_w"].T, f["L0_tok_W_embed"], f["L0_tok_b_patch"], f["L0_tok_b_embed"], f["L0_tok_ln_gamma"],
               f["L0_tok_ln_beta"], f["L0_tok_b_out"], f["L0_attn_bq"], f["L0_attn_bk"], f["L0_attn_ocr_bias"], f["L0_attn_bo"],
               f["L0_tok_b_coord"], f["L0_tok_b_spinor"], f["L0_ffn_bias"], bv, f["L0_tok_pos_embed"][0].T]
    weights = np.concatenate([_rows(a) for a in columns], axis=1)

    def up(shared, routed):
        both = np.concatenate([f[shared], f[routed]])
        return both.reshape(XP + 1, P, P).transpose(0, 2, 1)

    down = np.concatenate([f["L0_ffn_shared_w_down"], f["L0_ffn_w_down"]]).reshape(XP + 1, 2, P, FF).transpose(0, 1, 3, 2).reshape(XP + 1, P, P)
    experts = np.concatenate([up("L0_ffn_shared_w_gate", "L0_ffn_w_gate"), up("L0_ffn_shared_w_up", "L0_ffn_w_up"), down], axis=2)
    arrays = {"patches": patches, "w_patch": w_patch, "weights": weights, "consts": _constants(), "experts": experts}
    arrays = {k: np.ascontiguousarray(v) for k, v in arrays.items()}

    nc = _bacc.Bacc("TRN2", target_bir_lowering=False, num_devices=1)
    args = [nc.dram_tensor(k, v.shape, F32, kind="ExternalInput").ap() for k, v in arrays.items()]
    args.append(nc.dram_tensor("gate_scratch", (E, N), F32, kind="Internal").ap())
    args.append(nc.dram_tensor("out", (P, N), F32, kind="ExternalOutput").ap())
    build(nc, *args)
    r = _run(nc, [arrays], core_ids=[0])
    return np.ascontiguousarray(np.asarray(r.results[0]["out"]).T).reshape(IMAGES, SEQ, P)
```

```python
from contextlib import ExitStack

import numpy as np

import concourse.bass as bass
from concourse import mybir

F32 = mybir.dt.float32
F32R = mybir.dt.float32r
ACT = mybir.ActivationFunctionType
ALU = mybir.AluOpType
AX_X = mybir.AxisListType.X

P = 128
IMAGES, CHANNELS, IMG, PATCH = 32, 3, 112, 16
GRID = IMG // PATCH
SEQ = GRID * GRID
N = IMAGES * SEQ
KT = CHANNELS * PATCH * PATCH // P
DC, DS = 8, 4
HEADS, HD = 8, 16
HP = HEADS // 2
WINDOW = 5
E, FF, TOPK, SHARED = 64, 64, 6, 2
CAPACITY = max(1, int(N * TOPK * 2.0 / E))
EPS = 1e-5

CH = 4
CI = IMAGES // CH
CW = CI * SEQ
PW = 2 * SEQ
PAIRS = IMAGES // 2
TILES = CW // PW
QW = 64
XP = E // 2
LAG = 3
SENTINEL = -3.0e38

W_SPINCO, W_OUT, W_Q, W_K, W_V, W_O, W_ROUTER, W_EMBED = 0, 40, 168, 296, 424, 552, 1064, 1128
V0 = W_EMBED + 128
CO_AT = 32
(V_PATCH, V_EMBED, V_GAMMA, V_BETA, V_OUT, V_BQ, V_BK, V_OCR, V_BO, V_COORD, V_SPIN,
 V_ROUTER, V_BV) = range(V0, V0 + 13)
W_POS = V0 + 14
WCOLS = W_POS + SEQ
C_IDENT, C_CENTER, C_MEAN, C_ONES, C_BANDQ = 0, 128, 256, 384, 512
C_BANDK, C_PARITY, C_IMAGE, C_EPS = 640, 640 + CW, 642 + CW, 644 + CW
C_HP = C_EPS + 1
CCOLS = C_HP + HP


def build(nc, patches, w_patch, weights, consts, experts, gate_scratch, out):
    ctx = ExitStack()
    with ctx:
        def sb(name, shape, dt=F32):
            return ctx.enter_context(nc.sbuf_tensor(name, shape, dt))

        def sem(name):
            return ctx.enter_context(nc.semaphore(name))

        wpatch = sb("wpatch", [P, KT, P])
        wts = sb("wts", [P, WCOLS])
        cst = sb("cst", [P, CCOLS])
        pat = sb("pat", [P, KT, N])
        posb = sb("posb", [P, SEQ])
        x0 = sb("x0", [P, CH, CW])
        coords = sb("coords", [DC, CH, CW])
        spin2 = sb("spin2", [DS, CH, CW])
        xman = sb("xman", [P, CH, CW])
        xenh = sb("xenh", [P, CH, CW])
        sq = sb("sq", [P, CH, CW])
        xmk = sq
        logvar = sq
        rstd2 = sq
        rstd = sb("rstd", [P, CH, CW])
        ynorm = x0
        h1 = sb("h1", [P, N])
        xn = sb("xn", [P, N])
        btok = sb("btok", [P, 1])
        ghalf = sb("ghalf", [P, 1])
        bproj = sb("bproj", [P, 1])
        bq1 = sb("bq1", [P, 1])
        qbias = sb("qbias", [P, 1])
        qT = xenh
        kT = xman
        bandq = sb("bandq", [PW, P], F32R)
        bandk = sb("bandk", [PW, CW], F32R)
        xpair = sb("xpair", [P, 2, PW])
        khead = sb("khead", [P, 2, 2, HP, SEQ])
        qdiag = sb("qdiag", [P, 2, 2, 2, QW])
        vdiag = sb("vdiag", [PW, 2, HP, 2, 2 * HD])
        smax = sb("smax", [P, 2, HEADS])
        sshift = sb("sshift", [P, 2, CW])
        probs = sb("probs", [P, 2, HP, 2, SEQ])
        ssum = sb("ssum", [P, 2, HEADS])
        rsum = sb("rsum", [P, 2, HEADS])
        probsT = sb("probsT", [PW, 2, HP * P])
        onorm = sb("onorm", [P, 2, 2 * HP * HD])
        oT = sb("oT", [P, 2, TILES, SEQ])
        h2 = sb("h2", [P, N])
        x2 = x0
        x2h = sb("x2h", [P, CH, CW], F32R)
        x2l = sb("x2l", [P, CH, CW], F32R)
        logT = xenh[0:E, :, :]
        logits = sb("logits", [PW, CH, TILES, E + 2])
        top8 = sb("top8", [PW, CH, TILES, 8])
        top6 = sb("top6", [PW, CH, TILES, 8])
        marked = sb("marked", [PW, CH, TILES, E + 2])
        negmax = sb("negmax", [PW, CH, TILES])
        lexp = sb("lexp", [PW, CH, TILES, E])
        lsel = sb("lsel", [PW, CH, TILES, E])
        lsum = sb("lsum", [PW, CH, 4, TILES])
        gsel = sb("gsel", [PW, CH, TILES, 2 * E])
        gT = pat[0:E, 2, :].rearrange("p (a b) -> p a b", a=CH)
        selT = pat[0:E, 3, :].rearrange("p (a b) -> p a b", a=CH)
        rank = pat[0:E, 4, :].rearrange("p (a b) -> p a b", a=CH)
        ones_row = sb("ones_row", [E, CW])
        gateT = pat[0:E, 5, :].rearrange("p (a b) -> p a b", a=CH)
        wraw = sb("wraw", [P, 2, 3 * P])
        wh = sb("wh", [P, 2, 3 * P], F32R)
        wl = sb("wl", [P, 2, 3 * P], F32R)
        half = sb("half", [P, CW])
        gbc = pat[:, 0:2, :]
        act_g = sb("act_g", [P, 2, CW])
        prod = sb("prod", [P, 2, CW])
        hid = sb("hid", [P, 2, CW])
        hidh = sb("hidh", [P, CH, CW], F32R)
        hidl = sb("hidl", [P, CH, CW], F32R)
        result = xman

        bank = [ctx.enter_context(nc.psum_tensor(f"bank{i}", [P, 512], F32)) for i in range(8)]
        bA, bB = bank[0:4], bank[4:8]
        b_qk, b_v, b_s, b_pT, b_o, b_oT, b_proj = bank[0], bank[1], bank[2:4], bank[4], bank[5], bank[6], bank[7]

        s_wpatch, s_weights, s_consts = sem("wpatch_in"), sem("weights_in"), sem("consts_in")
        s_pat = [sem(f"patches_in{c}") for c in range(CH)]
        posb_ready, biasmm_ready, bias_ready = sem("posb_ready"), sem("biasmm_ready"), sem("bias_ready")
        half_ready, ghalf_ready = sem("half_ready"), sem("ghalf_ready")
        bq1_ready, qbias_ready, band_ready = sem("bq1_ready"), sem("qbias_ready"), sem("band_ready")
        pads_ready = sem("pads_ready")
        x0_mm, x0_ready = sem("x0_mm"), sem("x0_ready")
        cs_mm, spinco_ready = sem("cs_mm"), sem("spinco_ready")
        man_mm, xman_ready, xmk_ready, xenh_ready = sem("man_mm"), sem("xman_ready"), sem("xmk_ready"), sem("xenh_ready")
        cen_mm = [sem(f"cen_mm{n}") for n in range(3)]
        sq_ready = [sem(f"sq_ready{n}") for n in range(3)]
        var_mm = [sem(f"var_mm{n}") for n in range(3)]
        logvar_ready = [sem(f"logvar_ready{n}") for n in range(3)]
        rstd2_ready = [sem(f"rstd2_ready{n}") for n in range(3)]
        refine_step = [sem(f"refine_step{n}") for n in range(3)]
        rstd_ready = [sem(f"rstd_ready{n}") for n in range(3)]
        norm_ready = [sem(f"norm_ready{n}") for n in range(3)]
        qk_mm, qk_ready = sem("qk_mm"), sem("qk_ready")
        h1_mm, h1_ready = sem("h1_mm"), sem("h1_ready")
        xpair_ready, qdiag_ready, khead_ready, v_mm, vdiag_ready = (
            sem("xpair_ready"), sem("qdiag_ready"), sem("khead_ready"), sem("v_mm"), sem("vdiag_ready"))
        scores_mm, smax_ready, sshift_ready, probs_ready, ssum_ready, rsum_ready = (
            sem("scores_mm"), sem("smax_ready"), sem("sshift_ready"), sem("probs_ready"), sem("ssum_ready"), sem("rsum_ready"))
        pT_mm, probsT_ready, o_mm, onorm_ready, oT_mm, oT_ready, proj_mm, h2_ready = (
            sem("pT_mm"), sem("probsT_ready"), sem("o_mm"), sem("onorm_ready"), sem("oT_mm"), sem("oT_ready"), sem("proj_mm"), sem("h2_ready"))
        x2h_ready, x2l_ready = sem("x2h_ready"), sem("x2l_ready")
        logT_mm, logT_ready, logits_mm, logits_ready = sem("logT_mm"), sem("logT_ready"), sem("logits_mm"), sem("logits_ready")
        top8_ready, negmax_ready, top6_ready, marked_ready, chosen_ready, lexp_ready, lsel_ready, lsum_step = (
            sem("top8_ready"), sem("negmax_ready"), sem("top6_ready"), sem("marked_ready"), sem("chosen_ready"), sem("lexp_ready"),
            sem("lsel_ready"), sem("lsum_step"))
        gsel_ready, gT_mm, gT_ready, selT_ready, rank_ready, gateT_ready, gate_stored = (
            sem("gsel_ready"), sem("gT_mm"), sem("gT_ready"), sem("selT_ready"), sem("rank_ready"), sem("gateT_ready"), sem("gate_stored"))
        s_wraw = [sem(f"expert_in{s}") for s in range(2)]
        s_gbc = [sem(f"gates_in{s}") for s in range(2)]
        wgu_high, wgu_low, wd_high, wd_low = sem("wgu_high"), sem("wgu_low"), sem("wd_high"), sem("wd_low")
        hidh_ready, hidl_ready = sem("hidh_ready"), sem("hidl_ready")
        gu_mm, actg_ready, prod_ready, hid_ready, down_mm = sem("gu_mm"), sem("actg_ready"), sem("prod_ready"), sem("hid_ready"), sem("down_mm")
        result_ready, s_out = sem("result_ready"), sem("out_stored")

        def w(a, n, rows=P):
            return wts[0:rows, a:a + n]

        def c_(a, n, rows=P):
            return cst[0:rows, a:a + n]

        ident = c_(C_IDENT, P)
        qflat, kflat = qT[:, :, :].rearrange("p a b -> p (a b)"), kT[:, :, :].rearrange("p a b -> p (a b)")
        chunk = [slice(c * CW, (c + 1) * CW) for c in range(CH)]

        def bcast(ap, axis, count):
            ap = ap.unsqueeze(axis)
            shape = list(ap.shape)
            shape[axis] = count
            return ap.to_broadcast(shape)

        def waves(stages):
            return [(n - c, c) for n in range(stages + CH - 1) for c in reversed(range(CH)) if 0 <= n - c < stages]

        TOK_STAGES, ROUTER_STAGES = 9, 6

        block = ctx.enter_context(nc.Block())

        @block.sync
        def _(sp):
            sp.dma_start(wpatch[:, :, :], w_patch).then_inc(s_wpatch, 16)
            sp.dma_start(pat[:, :, chunk[0]], patches[:, :, chunk[0]]).then_inc(s_pat[0], 16)
            sp.dma_start(wts[:, :], weights).then_inc(s_weights, 16)
            sp.dma_start(cst[:, :], consts).then_inc(s_consts, 16)
            for c in range(1, CH):
                sp.dma_start(pat[:, :, chunk[c]], patches[:, :, chunk[c]]).then_inc(s_pat[c], 16)
            for s in range(2):
                sp.dma_start(wraw[:, s, :], experts[s]).then_inc(s_wraw[s], 16)
            for c in range(CH):
                sp.wait_ge(gateT_ready, c + 1)
                sp.dma_start(gate_scratch[:, chunk[c]], gateT[:, c, :]).then_inc(gate_stored, 16)
            sp.wait_ge(gate_stored, 16 * CH)

            def load_gates(j, s):
                sp.dma_start(gbc[:, s, :], bcast(gate_scratch[bass.ds(2 * j, 2), :], 1, FF)).then_inc(s_gbc[s], 16)

            def refill_weights(p, s):
                sp.wait_ge(wgu_low, p - 1)
                sp.wait_ge(wd_low, p - 1)
                sp.dma_start(wraw[:, s, :], experts[bass.ds(p, 1), :, :].rearrange("a p n -> p (a n)")).then_inc(s_wraw[s], 16)

            def refill_gates(j, s):
                sp.wait_ge(hid_ready, CH * j)
                load_gates(j, s)

            load_gates(0, 0)
            refill_weights(2, 0)
            load_gates(1, 1)
            refill_weights(3, 1)
            with sp.Fori(0, (XP - 4) // 2) as r:
                q = 2 + 2 * r
                for v in range(2):
                    refill_gates(q + v, v)
                    refill_weights(q + v + 2, v)
            for v in range(2):
                refill_gates(XP - 2 + v, v)
                if v == 0:
                    refill_weights(XP, 0)
            for c in range(CH):
                sp.wait_ge(result_ready, c + 1)
                sp.dma_start(out[:, chunk[c]], result[:, c, :]).then_inc(s_out, 16)
            sp.wait_ge(s_out, 16 * CH)

        @block.tensor
        def _(pe):
            pe.wait_ge(s_wpatch, 16)

            def patch_product(c):
                pe.wait_ge(s_pat[c], 16)
                for k in range(KT):
                    last = pe.matmul(bA[c][:, 0:CW], wpatch[:, k, :], pat[:, k, chunk[c]], start=(k == 0), stop=(k == KT - 1))
                last.then_inc(x0_mm, 1)

            def folded_biases():
                pe.wait_ge(s_weights, 16)
                pe.matmul(bB[3][:, 0:1], w(W_OUT, P), w(V_BETA, 1), start=True, stop=True)
                for t in range(2):
                    last = pe.matmul(bB[3][:, 1:2], w(W_O + t * P, P), w(V_BV + t, 1), start=(t == 0), stop=(t == 1))
                last.then_inc(biasmm_ready, 1)

            def spinors_coordinates(c):
                if c == 0:
                    folded_biases()
                    pe.wait_ge(s_consts, 16)
                if c == 3:
                    pe.wait_ge(bias_ready, 2)
                pe.wait_ge(x0_ready, c + 1)
                pe.matmul(bB[c][0:CO_AT + DC, 0:CW], w(W_SPINCO, CO_AT + DC), x0[:, c, :], start=True, stop=True).then_inc(cs_mm, 1)

            def manifold(c):
                pe.wait_ge(spinco_ready, c + 1)
                pe.matmul(bA[c][:, 0:CW], w(W_EMBED, P, DC), coords[:, c, :], start=True, stop=True)
                pe.matmul(bB[c][:, 0:CW], c_(C_ONES, P, DS), spin2[:, c, :], start=True, stop=True).then_inc(man_mm, 1)

            def centre(n, c, src, ready):
                pe.wait_ge(ready, c + 1)
                pe.matmul(bA[c][:, 0:CW], c_(C_CENTER, P), src, start=True, stop=True).then_inc(cen_mm[n], 1)

            def variance(n, c):
                pe.wait_ge(sq_ready[n], c + 1)
                pe.matmul(bB[c][:, 0:CW], c_(C_MEAN, P), sq[:, c, :], start=True, stop=True).then_inc(var_mm[n], 1)

            def tokenizer_out(c):
                pe.wait_ge(norm_ready[0], c + 1)
                pe.matmul(bB[c][:, 0:CW], w(W_OUT, P), ynorm[:, c, :], start=True, stop=True).then_inc(h1_mm, 1)

            def queries_keys(c):
                pe.wait_ge(norm_ready[1], c + 1)
                pe.matmul(bA[c][:, 0:CW], w(W_Q, P), xn[:, chunk[c]], start=True, stop=True)
                pe.matmul(bB[c][:, 0:CW], w(W_K, P), xn[:, chunk[c]], start=True, stop=True).then_inc(qk_mm, 1)

            stages = (patch_product, spinors_coordinates, manifold, lambda c: centre(0, c, xenh[:, c, :], xenh_ready),
                      lambda c: variance(0, c), tokenizer_out, lambda c: centre(1, c, h1[:, chunk[c]], h1_ready),
                      lambda c: variance(1, c), queries_keys)
            for k, c in waves(TOK_STAGES):
                stages[k](c)

            def project_v(j, s, n):
                pe.wait_ge(xpair_ready, j + 1)
                if n >= 1:
                    pe.wait_ge(vdiag_ready, j)
                pe.matmul(b_v[0:PW, 0:P], xpair[:, s, :], w(W_V, P), start=True, stop=True).then_inc(v_mm, 1)

            def scores(j, s, n):
                pe.wait_ge(qdiag_ready, j + 1)
                pe.wait_ge(khead_ready, j + 1)
                if n >= 2:
                    pe.wait_ge(sshift_ready, j - 1)
                pe.matmul(b_s[s][:, 0:CW], bandq[:, :], bandk[:, :], start=True, stop=False)
                for m in range(2):
                    last = pe.matmul(b_s[s][:, 0:CW].rearrange("p (h m k) -> p h m k", h=HP, m=2)[:, :, m, :],
                                     qdiag[:, s, m, :, :].rearrange("p a b -> p (a b)"), khead[:, s, m, :, :], start=False, stop=(m == 1))
                last.then_inc(scores_mm, 1)

            def transpose_probs(j, s, n):
                pe.wait_ge(probs_ready, j + 1)
                if n >= 1:
                    pe.wait_ge(probsT_ready, j)
                for hp in range(HP):
                    last = pe.transpose(b_pT[0:PW, hp * P:(hp + 1) * P], probs[:, s, hp, :, :].rearrange("p a b -> p (a b)"), ident)
                last.then_inc(pT_mm, 1)

            def weigh_values(j, s, n):
                pe.wait_ge(probsT_ready, j + 1)
                pe.wait_ge(vdiag_ready, j + 1)
                if n >= 1:
                    pe.wait_ge(onorm_ready, j)
                for hp in range(HP):
                    last = pe.matmul(b_o[:, hp * 64:(hp + 1) * 64], probsT[:, s, hp * P:(hp + 1) * P],
                                     vdiag[:, s, hp, :, :].rearrange("p a b -> p (a b)"), start=True, stop=True)
                last.then_inc(o_mm, 1)

            def transpose_out(j, s, n):
                pe.wait_ge(onorm_ready, j + 1)
                if n >= 1:
                    pe.wait_ge(oT_ready, j)
                pe.transpose(b_oT[:, 0:P], onorm[:, s, :], ident).then_inc(oT_mm, 1)

            def project_out(c, first):
                pe.wait_ge(oT_ready, TILES * (c + 1))
                if not first:
                    pe.wait_ge(h2_ready, c)
                for m in range(2):
                    for t in range(2):
                        last = pe.matmul(b_proj[:, 0:CW].rearrange("p (u m q) -> p u m q", u=TILES, m=2)[:, :, m, :], w(W_O + (2 * m + t) * P, P),
                                         oT[:, t, :, :], start=(t == 0), stop=(t == 1))
                last.then_inc(proj_mm, 1)

            def attend(j, n):
                if 1 <= n <= PAIRS:
                    transpose_probs(j - 1, (n - 1) % 2, n - 1)
                if n < PAIRS:
                    scores(j, n % 2, n)
                    project_v(j, n % 2, n)
                if 1 <= n <= PAIRS:
                    weigh_values(j - 1, (n - 1) % 2, n - 1)
                if n >= 2:
                    transpose_out(j - 2, n % 2, n - 2)

            pe.wait_ge(qk_ready, CH)
            pe.wait_ge(band_ready, 2)
            for n in range(TILES):
                attend(n, n)
            with pe.Fori(0, CH - 1) as r:
                for u in range(TILES):
                    attend(TILES * r + (TILES + u), TILES + u)
                    if u == 1:
                        project_out(r, False)
            for n in (PAIRS, PAIRS + 1):
                attend(n, n)
            project_out(CH - 1, False)

            def router_logits(c):
                pe.wait_ge(norm_ready[2], c + 1)
                pe.matmul(bA[c][0:E, 0:CW], w(W_ROUTER, E), x2[:, c, :], start=True, stop=True).then_inc(logT_mm, 1)

            def logits_by_token(c):
                pe.wait_ge(logT_ready, c + 1)
                for t in range(TILES):
                    last = pe.transpose(bB[c][0:PW, t * E:(t + 1) * E], logT[:, c, t * PW:(t + 1) * PW], c_(C_IDENT, E, E))
                last.then_inc(logits_mm, 1)

            def gates_by_expert(c):
                pe.wait_ge(gsel_ready, c + 1)
                for t in range(TILES):
                    last = pe.transpose(bA[c][:, t * PW:(t + 1) * PW], gsel[:, c, t, :], c_(C_IDENT, PW, PW))
                last.then_inc(gT_mm, 1)

            pe.wait_ge(h2_ready, CH)
            stages = (lambda c: centre(2, c, h2[:, chunk[c]], h2_ready), lambda c: variance(2, c), router_logits, logits_by_token,
                      None, gates_by_expert)
            for k, c in waves(ROUTER_STAGES):
                if stages[k]:
                    stages[k](c)

            def gate_up(k, p, c, hs, first=False):
                g, u = bB[2 * (c % 2)], bB[2 * (c % 2) + 1]
                if c == 0:
                    pe.wait_ge(wgu_low, p + 1)
                if not first:
                    pe.wait_ge(prod_ready, k - 1)
                for b, a in ((g, 0), (u, P)):
                    pe.matmul(b[:, 0:CW], wh[:, hs, a:a + P], x2h[:, c, :], start=True, stop=False)
                    pe.matmul(b[:, 0:CW], wh[:, hs, a:a + P], x2l[:, c, :], start=False, stop=False)
                    last = pe.matmul(b[:, 0:CW], wl[:, hs, a:a + P], x2h[:, c, :], start=False, stop=True)
                last.then_inc(gu_mm, 1)

            def down(k, p, c, hs):
                if c == 0:
                    pe.wait_ge(wd_low, p + 1)
                pe.wait_ge(hidl_ready, k + 1)
                a = 2 * P
                for x, y in ((wh, hidh), (wh, hidl), (wl, hidh)):
                    last = pe.matmul(bA[c][:, 0:CW], x[:, hs, a:a + P], y[:, c, :], start=False, stop=True, skip_group_check=True)
                last.then_inc(down_mm, 1)

            pe.wait_ge(x2l_ready, CH)
            pe.wait_ge(logits_ready, CH)
            for c in range(CH):
                gate_up(c, 0, c, 0, first=(c < 2))
                if c == 1:
                    for a in range(CH):
                        pe.wait_ge(gT_ready, a + 1)
                        pe.matmul(bA[a][:, 0:CW], ident, h2[:, chunk[a]], start=True, stop=True)
                if c >= LAG:
                    down(c - LAG, 0, c - LAG, 0)
            with pe.Fori(0, XP // 2) as r:
                for v in range(2):
                    p = 2 * r + (v + 1)
                    for c in range(CH):
                        gate_up(CH * p + c, p, c, (v + 1) % 2)
                        back = c - LAG
                        if back < 0:
                            down(CH * p + back, p - 1, back + CH, v)
                        else:
                            down(CH * p + back, p, back, (v + 1) % 2)
            for c in range(CH - LAG, CH):
                down(CH * XP + c, XP, c, XP % 2)

        @block.scalar
        def _(act):
            act.preload_act_table_set("natural_log_exp_and_others")
            act.wait_ge(s_weights, 16)
            act.wait_ge(s_consts, 16)

            def take_spinco(c):
                act.wait_ge(cs_mm, c + 1)
                act.activation(spin2[:, c, :], bB[c][0:DS, 0:CW], ACT.Square, bias=w(V_SPIN, 1, DS))
                act.activation(coords[:, c, :], bB[c][CO_AT:CO_AT + DC, 0:CW], ACT.Identity, bias=w(V_COORD, 1, DC)).then_inc(spinco_ready, 1)

            def take_manifold(c):
                act.wait_ge(man_mm, c + 1)
                act.activation(xman[:, c, :], bA[c][:, 0:CW], ACT.Identity, bias=w(V_EMBED, 1)).then_inc(xman_ready, 1)

            def squares(n, c):
                act.wait_ge(cen_mm[n], c + 1)
                act.activation(sq[:, c, :], bA[c][:, 0:CW], ACT.Square).then_inc(sq_ready[n], 1)

            def deviation(n, c):
                act.wait_ge(var_mm[n], c + 1)
                act.activation(logvar[:, c, :], bB[c][:, 0:CW], ACT.Ln, bias=c_(C_EPS, 1)).then_inc(logvar_ready[n], 1)
                act.wait_ge(logvar_ready[n], c + 1)
                act.activation(rstd[:, c, :], logvar[:, c, :], ACT.Exp, scale=-0.5).then_inc(rstd_ready[n], 1)
                act.wait_ge(rstd_ready[n], c + 1)
                act.activation(rstd2[:, c, :], rstd[:, c, :], ACT.Square).then_inc(rstd2_ready[n], 1)

            def take_h1(c):
                if c == 0:
                    act.wait_ge(bias_ready, 2)
                act.wait_ge(h1_mm, c + 1)
                act.activation(h1[:, chunk[c]], bB[c][:, 0:CW], ACT.Identity, bias=btok[:, :]).then_inc(h1_ready, 1)

            def take_qk(c):
                if c == 0:
                    act.wait_ge(qbias_ready, 1)
                act.wait_ge(qk_mm, c + 1)
                act.activation(qT[:, c, :], bA[c][:, 0:CW], ACT.Identity, bias=qbias[:, :], scale=1.0 / HD ** 0.5)
                act.activation(kT[:, c, :], bB[c][:, 0:CW], ACT.Identity, bias=w(V_BK, 1)).then_inc(qk_ready, 1)

            stages = (None, take_spinco, take_manifold, lambda c: squares(0, c), lambda c: deviation(0, c), take_h1,
                      lambda c: squares(1, c), lambda c: deviation(1, c), take_qk)
            for k, c in waves(TOK_STAGES):
                if stages[k]:
                    stages[k](c)

            def take_probsT(j, s, n):
                act.wait_ge(pT_mm, j + 1)
                if n >= 2:
                    act.wait_ge(o_mm, j - 1)
                act.activation(probsT[:, s, :], b_pT[0:PW, :], ACT.Identity).then_inc(probsT_ready, 1)

            def exponentials(j, s, n):
                act.wait_ge(sshift_ready, j + 1)
                if n >= 2:
                    act.wait_ge(pT_mm, j - 1)
                    act.wait_ge(ssum_ready, j - 1)
                act.activation(probs[:, s, :, :, :].rearrange("p a b c -> p (a b c)"), sshift[:, s, :], ACT.Exp).then_inc(probs_ready, 1)

            def take_oT(j, n):
                act.wait_ge(oT_mm, j + 1)
                act.activation(oT[:, :, n % TILES, :], b_oT[:, 0:P].rearrange("p (t q) -> p t q", t=2)[:, :, 0:SEQ], ACT.Identity).then_inc(oT_ready, 1)

            def attend(j, n):
                if 1 <= n <= PAIRS:
                    take_probsT(j - 1, (n - 1) % 2, n - 1)
                if n < PAIRS:
                    exponentials(j, n % 2, n)
                if n >= 2:
                    take_oT(j - 2, n - 2)

            for n in range(TILES):
                attend(n, n)
            with act.Fori(0, CH - 1) as r:
                for u in range(TILES):
                    if u == 2:
                        act.wait_ge(proj_mm, r + 1)
                    attend(TILES * r + (TILES + u), TILES + u)
            for n in (PAIRS, PAIRS + 1):
                attend(n, n)

            def take_logT(c):
                act.wait_ge(norm_ready[2], c + 1)
                act.activation(x2h[:, c, :], x2[:, c, :], ACT.Copy).then_inc(x2h_ready, 1)
                act.wait_ge(logT_mm, c + 1)
                act.activation(logT[:, c, :], bA[c][0:E, 0:CW], ACT.Identity, bias=w(V_ROUTER, 1, E)).then_inc(logT_ready, 1)

            def take_logits(c):
                act.wait_ge(logits_mm, c + 1)
                act.activation(logits[:, c, :, 0:E], bB[c][0:PW, 0:TILES * E].rearrange("p (a b) -> p a b", a=TILES), ACT.Identity).then_inc(logits_ready, 1)
                act.wait_ge(negmax_ready, c + 1)
                for t in range(TILES):
                    last = act.activation(lexp[:, c, t, :], logits[:, c, t, 0:E], ACT.Exp, bias=negmax[:, c, t:t + 1], accum_out=lsum[:, c, 0, t:t + 1])
                last.then_inc(lexp_ready, 1)

            def take_gT(c):
                act.wait_ge(gT_mm, c + 1)
                act.activation(selT[:, c, :], bA[c][E:2 * E, 0:CW], ACT.Identity).then_inc(selT_ready, 1)
                act.activation(gT[:, c, :], bA[c][0:E, 0:CW], ACT.Identity).then_inc(gT_ready, 1)

            def split_gate_up(p, hs, first=False):
                act.wait_ge(s_wraw[hs], 8 * (p - hs) + 16)
                if not first:
                    act.wait_ge(gu_mm, CH * (p - 1))
                act.activation(wh[:, hs, 0:2 * P], wraw[:, hs, 0:2 * P], ACT.Copy).then_inc(wgu_high, 1)

            def split_down(p, hs, first=False):
                if not first:
                    act.wait_ge(down_mm, CH * (p - 1))
                act.activation(wh[:, hs, 2 * P:3 * P], wraw[:, hs, 2 * P:3 * P], ACT.Copy).then_inc(wd_high, 1)

            for p in range(2):
                split_gate_up(p, p, True)
                split_down(p, p, True)
            stages = (lambda c: squares(2, c), lambda c: deviation(2, c), take_logT, take_logits, None, take_gT)
            for k, c in waves(ROUTER_STAGES):
                if stages[k]:
                    stages[k](c)

            def silu(k, c, first=False):
                act.wait_ge(gu_mm, k + 1)
                if not first:
                    act.wait_ge(prod_ready, k - 1)
                act.activation(act_g[:, c % 2, :], bB[2 * (c % 2)][:, 0:CW], ACT.Silu).then_inc(actg_ready, 1)

            def high(k, c, first=False):
                act.wait_ge(hid_ready, k + 1)
                if not first:
                    act.wait_ge(down_mm, k - CH + 1)
                act.activation(hidh[:, c, :], hid[:, c % 2, :], ACT.Copy).then_inc(hidh_ready, 1)

            def expert_turns(p, hs, last=False, shared=False):
                for c in range(CH):
                    silu(CH * p + c, c, shared and c < 2)
                    if not (shared and c == 0):
                        high(CH * p + (c - 1), (c - 1) % CH, shared)
                    if not shared and not last:
                        if c == 1:
                            split_gate_up(p + 1, 1 - hs)
                        if c == 3:
                            split_down(p + 1, 1 - hs)

            expert_turns(0, 0, shared=True)
            with act.Fori(0, XP // 2 - 1) as r:
                for v in range(2):
                    expert_turns(2 * r + (v + 1), 1 - v)
            expert_turns(XP - 1, 1)
            expert_turns(XP, 0, last=True)
            high(CH * XP + CH - 1, CH - 1)

        @block.vector
        def _(dve):
            dve.wait_ge(s_weights, 16)
            dve.tensor_scalar(posb[:, :], w(W_POS, SEQ), w(V_PATCH, 1), None, ALU.add).then_inc(posb_ready, 1)
            dve.tensor_tensor(bq1[:, :], w(V_BQ, 1), w(V_OCR, 1), ALU.add).then_inc(bq1_ready, 1)
            dve.wait_ge(s_consts, 16)
            dve.tensor_copy(bandq[:, :], c_(C_BANDQ, P, PW)).then_inc(band_ready, 1)
            dve.tensor_copy(bandk[:, :], c_(C_BANDK, CW, PW)).then_inc(band_ready, 1)
            dve.tensor_scalar(ghalf[:, :], w(V_GAMMA, 1), -0.5, None, ALU.mult).then_inc(ghalf_ready, 1)
            dve.wait_ge(ghalf_ready, 1)
            dve.wait_ge(bq1_ready, 1)
            dve.tensor_scalar(qbias[:, :], bq1[:, :], 1.0 / HD ** 0.5, None, ALU.mult).then_inc(qbias_ready, 1)

            def embed(c):
                if c == 0:
                    dve.wait_ge(posb_ready, 1)
                dve.wait_ge(x0_mm, c + 1)
                dve.tensor_tensor(x0[:, c, :].rearrange("p (a b) -> p a b", a=CI), bA[c][:, 0:CW].rearrange("p (a b) -> p a b", a=CI),
                                  bcast(posb[:, :], 1, CI), ALU.add).then_inc(x0_ready, 1)
                if c == 0:
                    dve.wait_ge(biasmm_ready, 1)
                    dve.tensor_tensor(btok[:, :], bB[3][:, 0:1], w(V_OUT, 1), ALU.add).then_inc(bias_ready, 1)
                    dve.tensor_tensor(bproj[:, :], bB[3][:, 1:2], w(V_BO, 1), ALU.add).then_inc(bias_ready, 1)

            def enhance(c):
                dve.wait_ge(xman_ready, c + 1)
                dve.tensor_tensor(xmk[:, c, :], bB[c][:, 0:CW], xman[:, c, :], ALU.mult).then_inc(xmk_ready, 1)
                dve.wait_ge(xmk_ready, c + 1)
                dve.tensor_tensor(xenh[:, c, :], xmk[:, c, :], x0[:, c, :], ALU.add).then_inc(xenh_ready, 1)

            def norm(n, c, out, factor):
                dve.wait_ge(rstd2_ready[n], c + 1)
                dve.scalar_tensor_tensor(rstd2[:, c, :], bB[c][:, 0:CW], c_(C_EPS, 1), rstd2[:, c, :], ALU.add, ALU.mult).then_inc(refine_step[n], 1)
                dve.wait_ge(refine_step[n], 2 * c + 1)
                dve.scalar_tensor_tensor(rstd[:, c, :], rstd2[:, c, :], -3.0, rstd[:, c, :], ALU.add, ALU.mult).then_inc(refine_step[n], 1)
                dve.wait_ge(refine_step[n], 2 * c + 2)
                dve.scalar_tensor_tensor(out, bA[c][:, 0:CW], factor, rstd[:, c, :], ALU.mult, ALU.mult).then_inc(norm_ready[n], 1)

            stages = (embed, None, enhance, None, lambda c: norm(0, c, ynorm[:, c, :], ghalf[:, :]), None, None, lambda c: norm(1, c, xn[:, chunk[c]], -0.5), None)
            for k, c in waves(TOK_STAGES):
                if stages[k]:
                    stages[k](c)

            def shift(j, s, n):
                dve.wait_ge(scores_mm, j + 1)
                sc = b_s[s][:, 0:CW].rearrange("p (a b) -> p a b", a=HEADS)
                dve.tensor_reduce(smax[:, s, :], sc, AX_X, ALU.max).then_inc(smax_ready, 1)
                dve.wait_ge(smax_ready, j + 1)
                if n >= 2:
                    dve.wait_ge(probs_ready, j - 1)
                dve.tensor_tensor(sshift[:, s, :].rearrange("p (a b) -> p a b", a=HEADS), sc, bcast(smax[:, s, :], 2, SEQ),
                                  ALU.subtract).then_inc(sshift_ready, 1)

            def take_v(j, s, n):
                dve.wait_ge(v_mm, j + 1)
                if n >= 2:
                    dve.wait_ge(o_mm, j - 1)
                v = b_v[0:PW, 0:P].rearrange("p (a b) -> p a b", a=HP)
                dve.tensor_tensor(vdiag[:, s, :, :, :], bcast(v, 2, 2), bcast(bcast(c_(C_IMAGE, 2, PW), 1, HP), 3, 2 * HD),
                                  ALU.mult).then_inc(vdiag_ready, 1)

            def sums(j, s):
                dve.wait_ge(probs_ready, j + 1)
                dve.tensor_reduce(ssum[:, s, :], probs[:, s, :, :, :].rearrange("p a b c -> p (a b) c"), AX_X, ALU.add).then_inc(ssum_ready, 1)
                dve.wait_ge(ssum_ready, j + 1)
                dve.reciprocal(rsum[:, s, :], ssum[:, s, :]).then_inc(rsum_ready, 1)

            def take_o(j, s, n):
                dve.wait_ge(o_mm, j + 1)
                dve.wait_ge(rsum_ready, j + 1)
                if n >= 2:
                    dve.wait_ge(oT_mm, j - 1)
                for t in range(2):
                    rows = slice(QW * t, QW * (t + 1))
                    o = b_o[rows, 0:4 * HP * HD].rearrange("p (h m t d) -> p h m t d", h=HP, m=2, t=2)[:, :, :, t, :]
                    r = rsum[rows, s, :].rearrange("p (h m) -> p h m", m=2)
                    last = dve.tensor_tensor(onorm[rows, s, :].rearrange("p (m h d) -> p h m d", m=2, h=HP), o, bcast(r, 3, HD), ALU.mult)
                last.then_inc(onorm_ready, 1)

            def residual(c):
                dve.wait_ge(proj_mm, c + 1)
                at = bass.ds(c * CW, CW)
                dve.scalar_tensor_tensor(h2[:, at], b_proj[:, 0:CW], bproj[:, :], h1[:, at], ALU.add, ALU.add).then_inc(h2_ready, 1)

            def attend(j, n):
                if n >= 2:
                    take_o(j - 2, n % 2, n - 2)
                if 1 <= n <= PAIRS:
                    sums(j - 1, (n - 1) % 2)
                if n < PAIRS:
                    shift(j, n % 2, n)
                    take_v(j, n % 2, n)

            for n in range(TILES):
                attend(n, n)
            with dve.Fori(0, CH - 1) as r:
                for u in range(TILES):
                    attend(TILES * r + (TILES + u), TILES + u)
                    if u == 1:
                        residual(r)
            for n in (PAIRS, PAIRS + 1):
                attend(n, n)
            residual(CH - 1)

            def choose(c):
                if c == 0:
                    dve.wait_ge(pads_ready, 4)
                dve.wait_ge(logits_ready, c + 1)
                for t in range(TILES):
                    last = dve.max(top8[:, c, t, :], logits[:, c, t, 0:E])
                last.then_inc(top8_ready, 1)
                dve.wait_ge(top8_ready, c + 1)
                dve.tensor_scalar(negmax[:, c, :], top8[:, c, :, 0], -1.0, None, ALU.mult).then_inc(negmax_ready, 1)
                dve.tensor_copy(top6[:, c, :, 0:TOPK], top8[:, c, :, 0:TOPK]).then_inc(top6_ready, 1)
                dve.wait_ge(top6_ready, c + 1)
                for t in range(TILES):
                    last = dve.match_replace(marked[:, c, t, :], top6[:, c, t, :], logits[:, c, t, :], -1.0e38)
                last.then_inc(marked_ready, 1)
                dve.wait_ge(marked_ready, c + 1)
                dve.tensor_tensor(gsel[:, c, :, E:2 * E], logits[:, c, :, 0:E], marked[:, c, :, 0:E], ALU.not_equal).then_inc(chosen_ready, 1)

            def gate_scale(c):
                dve.wait_ge(lsel_ready, c + 1)
                dve.tensor_reduce(lsum[:, c, 1, :], lsel[:, c, :, :], AX_X, ALU.add).then_inc(lsum_step, 1)
                dve.wait_ge(lsum_step, 3 * c + 1)
                dve.scalar_tensor_tensor(lsum[:, c, 2, :], lsum[:, c, 0, :], 1e-9, lsum[:, c, 1, :], ALU.mult, ALU.add).then_inc(lsum_step, 1)
                dve.wait_ge(lsum_step, 3 * c + 2)
                dve.reciprocal(lsum[:, c, 3, :], lsum[:, c, 2, :]).then_inc(lsum_step, 1)

            def admit(c):
                dve.wait_ge(selT_ready, c + 1)
                if c:
                    dve.wait_ge(rank_ready, c)
                dve.tensor_tensor_scan(rank[:, c, :], ones_row[:, :], selT[:, c, :], rank[:, c - 1, CW - 1:CW] if c else 0.0,
                                       ALU.mult, ALU.add).then_inc(rank_ready, 1)
                dve.wait_ge(rank_ready, c + 1)
                dve.wait_ge(gT_ready, c + 1)
                dve.scalar_tensor_tensor(gateT[:, c, :], rank[:, c, :], float(CAPACITY), gT[:, c, :], ALU.is_le, ALU.mult).then_inc(gateT_ready, 1)

            stages = (None, lambda c: norm(2, c, x2[:, c, :], -0.5), None, choose, gate_scale, admit)
            for k, c in waves(ROUTER_STAGES):
                if stages[k]:
                    stages[k](c)

            def times_up(k, c, first=False):
                dve.wait_ge(actg_ready, k + 1)
                if not first:
                    dve.wait_ge(hid_ready, k - 1)
                dve.tensor_tensor(prod[:, c % 2, :], bB[2 * (c % 2) + 1][:, 0:CW], act_g[:, c % 2, :], ALU.mult).then_inc(prod_ready, 1)

            def low(k, c, first=False):
                dve.wait_ge(hidh_ready, k + 1)
                if not first:
                    dve.wait_ge(down_mm, k - CH + 1)
                dve.tensor_tensor(hidl[:, c, :], hid[:, c % 2, :], hidh[:, c, :].bitcast(F32), ALU.subtract).then_inc(hidl_ready, 1)

            def expert_turns(p, shared=False):
                for c in range(CH):
                    times_up(CH * p + c, c, shared and c < 2)
                    if not (shared and c == 0):
                        low(CH * p + (c - 1), (c - 1) % CH, shared)

            expert_turns(0, shared=True)
            with dve.Fori(0, XP) as r:
                expert_turns(r + 1)
            low(CH * XP + CH - 1, CH - 1)
            for c in range(CH):
                dve.wait_ge(down_mm, CH * XP + c + 1)
                dve.tensor_copy(result[:, c, :], bA[c][:, 0:CW]).then_inc(result_ready, 1)

        @block.gpsimd
        def _(pool):
            pool.memset(qdiag[:, :, :, :, :], 0.0).then_inc(pads_ready, 1)
            pool.memset(logits[:, :, :, E:E + 2], SENTINEL).then_inc(pads_ready, 1)
            pool.memset(top6[:, :, :, TOPK:8], SENTINEL).then_inc(pads_ready, 1)
            pool.memset(ones_row[:, :], 1.0).then_inc(pads_ready, 1)
            pool.memset(half[:, :], 1.0 / SHARED).then_inc(half_ready, 1)

            def fetch_tokens(j, s, n):
                if n >= 2:
                    pool.wait_ge(v_mm, j - 1)
                pool.tensor_copy(xpair[:, s, :], xn[:, bass.ds(j * PW, PW)]).then_inc(xpair_ready, 1)

            def fetch_q(j, s, n):
                if n >= 2:
                    pool.wait_ge(scores_mm, j - 1)
                q = qflat[:, bass.ds(j * PW, PW)].rearrange("p (a b) -> p a b", a=2)
                pool.tensor_tensor(qdiag[:, s, :, :, 0:SEQ], bcast(q, 2, 2), bcast(bcast(c_(C_PARITY, 2), 1, 2), 3, SEQ),
                                   ALU.mult).then_inc(qdiag_ready, 1)

            def fetch_k(j, s, n):
                k = kflat[:, bass.ds(j * PW, PW)].rearrange("p (a b) -> p a b", a=2)
                pool.tensor_tensor(khead[:, s, :, :, :], bcast(k, 2, HP), bcast(bcast(c_(C_HP, HP), 1, 2), 3, SEQ),
                                   ALU.mult).then_inc(khead_ready, 1)

            def fetch(j, n):
                fetch_q(j, n % 2, n)
                fetch_k(j, n % 2, n)
                fetch_tokens(j, n % 2, n)

            pool.wait_ge(s_consts, 16)
            pool.wait_ge(pads_ready, 1)
            pool.wait_ge(qk_ready, CH)
            for n in range(2):
                fetch(n, n)
            with pool.Fori(0, PAIRS // 2 - 1) as r:
                for s in range(2):
                    fetch(2 * r + (2 + s), 2 + s)

            def split_gate_up(p, hs, first=False):
                pool.wait_ge(wgu_high, p + 1)
                if not first:
                    pool.wait_ge(gu_mm, CH * (p - 1))
                pool.tensor_tensor(wl[:, hs, 0:2 * P], wraw[:, hs, 0:2 * P], wh[:, hs, 0:2 * P].bitcast(F32), ALU.subtract).then_inc(wgu_low, 1)

            def split_down(p, hs, first=False):
                pool.wait_ge(wd_high, p + 1)
                if not first:
                    pool.wait_ge(down_mm, CH * (p - 1))
                pool.tensor_tensor(wl[:, hs, 2 * P:], wraw[:, hs, 2 * P:], wh[:, hs, 2 * P:].bitcast(F32), ALU.subtract).then_inc(wd_low, 1)

            for p in range(2):
                split_gate_up(p, p, True)
                split_down(p, p, True)

            def lower_x(c):
                pool.wait_ge(x2h_ready, c + 1)
                pool.tensor_tensor(x2l[:, c, :], x2[:, c, :], x2h[:, c, :].bitcast(F32), ALU.subtract).then_inc(x2l_ready, 1)

            def chosen_exp(c):
                pool.wait_ge(lexp_ready, c + 1)
                pool.wait_ge(chosen_ready, c + 1)
                pool.tensor_tensor(lsel[:, c, :, :], lexp[:, c, :, :], gsel[:, c, :, E:2 * E], ALU.mult).then_inc(lsel_ready, 1)

            def gates(c):
                pool.wait_ge(lsum_step, 3 * (c + 1))
                pool.tensor_tensor(gsel[:, c, :, 0:E], lsel[:, c, :, :], bcast(lsum[:, c, 3, :], 2, E), ALU.mult).then_inc(gsel_ready, 1)

            stages = (None, None, lower_x, chosen_exp, gates, None)
            for k, c in waves(ROUTER_STAGES):
                if stages[k]:
                    stages[k](c)

            def gated(k, c, gate, first=False):
                pool.wait_ge(prod_ready, k + 1)
                if not first:
                    pool.wait_ge(hidl_ready, k - 1)
                pool.tensor_tensor(hid[:, c % 2, :], prod[:, c % 2, :], gate, ALU.mult).then_inc(hid_ready, 1)

            def expert_turns(p, gs, last=False):
                pool.wait_ge(s_gbc[gs], 8 * (p - 1 - gs) + 16)
                for c in range(CH):
                    gated(CH * p + c, c, gbc[:, gs, chunk[c]])
                    if not last:
                        if c == 1:
                            split_gate_up(p + 1, gs)
                        if c == 3:
                            split_down(p + 1, gs)

            pool.wait_ge(half_ready, 1)
            for c in range(CH):
                gated(c, c, half[:, :], c < 2)
            with pool.Fori(0, XP // 2 - 1) as r:
                for v in range(2):
                    expert_turns(2 * r + (v + 1), v)
            expert_turns(XP - 1, 0)
            expert_turns(XP, 1, last=True)


def _constants():
    c = np.zeros((P, CCOLS), np.float32)
    c[:, C_IDENT:C_IDENT + P] = np.eye(P)
    c[:, C_CENTER:C_CENTER + P] = np.eye(P) - 1.0 / P
    c[:, C_MEAN:C_MEAN + P] = 1.0 / P
    c[:, C_ONES:C_ONES + P] = 1.0
    tenth = np.float32(0.1)
    high = np.float32(np.round(float(tenth) * 2 ** 15) / 2 ** 15)
    eye = np.eye(SEQ, dtype=np.float32)
    idx = np.arange(SEQ)
    band = (np.abs(idx[:, None] - idx[None, :]) <= WINDOW).astype(np.float32)
    for r, part in enumerate((high, tenth - high)):
        for t in range(2):
            c[r * SEQ:(r + 1) * SEQ, C_BANDQ + t * QW:C_BANDQ + t * QW + SEQ] = eye * part
        c[r * SEQ:(r + 1) * SEQ, C_BANDK:C_BANDK + CW] = np.tile(band, (1, HEADS))
    for t in range(2):
        c[:, C_PARITY + t] = (np.arange(P) // HD) % 2 == t
        c[t * SEQ:(t + 1) * SEQ, C_IMAGE + t] = 1.0
    c[:, C_EPS] = EPS
    for hp in range(HP):
        c[:, C_HP + hp] = np.arange(P) // (2 * HD) == hp
    return c


def _rows(a):
    a = np.asarray(a)
    a = a.reshape(a.shape[0], -1)
    return np.concatenate([a, np.zeros((P - a.shape[0], a.shape[1]), a.dtype)]) if a.shape[0] < P else a


def kernel(**inputs):
    import concourse.bacc as _bacc
    from concourse.bass_utils import run_bass_kernel_spmd as _run

    f = {k: np.asarray(v) for k, v in inputs.items()}
    patches = f["x"].reshape(IMAGES, CHANNELS, GRID, PATCH, GRID, PATCH).transpose(1, 3, 5, 0, 2, 4).reshape(KT, P, N).transpose(1, 0, 2)
    w_patch = f["L0_tok_W_patch"].reshape(KT, P, P).transpose(1, 0, 2)
    wo = f["L0_attn_Wo"].T.reshape(HP, 2, HD, P).transpose(0, 2, 1, 3).reshape(HP * HD, 2 * P)
    blank = np.zeros_like(wo)
    wo = np.concatenate([np.concatenate([wo, blank], axis=1), np.concatenate([blank, wo], axis=1)])
    bv = f["L0_attn_bv"].reshape(HP, 2, HD).transpose(0, 2, 1).reshape(HP * HD, 2)
    spinor = f["L0_tok_W_spinor"]
    columns = [spinor, np.zeros((P, CO_AT - DS), spinor.dtype), f["L0_tok_W_coord"], f["L0_tok_W_out"], f["L0_attn_Wq"].T, f["L0_attn_Wk"].T, f["L0_attn_Wv"].T,
               wo, f["L0_ffn_router_w"].T, f["L0_tok_W_embed"], f["L0_tok_b_patch"], f["L0_tok_b_embed"], f["L0_tok_ln_gamma"],
               f["L0_tok_ln_beta"], f["L0_tok_b_out"], f["L0_attn_bq"], f["L0_attn_bk"], f["L0_attn_ocr_bias"], f["L0_attn_bo"],
               f["L0_tok_b_coord"], f["L0_tok_b_spinor"], f["L0_ffn_bias"], bv, f["L0_tok_pos_embed"][0].T]
    weights = np.concatenate([_rows(a) for a in columns], axis=1)

    def up(shared, routed):
        both = np.concatenate([f[shared], f[routed]])
        return both.reshape(XP + 1, P, P).transpose(0, 2, 1)

    down = np.concatenate([f["L0_ffn_shared_w_down"], f["L0_ffn_w_down"]]).reshape(XP + 1, 2, P, FF).transpose(0, 1, 3, 2).reshape(XP + 1, P, P)
    experts = np.concatenate([up("L0_ffn_shared_w_gate", "L0_ffn_w_gate"), up("L0_ffn_shared_w_up", "L0_ffn_w_up"), down], axis=2)
    arrays = {"patches": patches, "w_patch": w_patch, "weights": weights, "consts": _constants(), "experts": experts}
    arrays = {k: np.ascontiguousarray(v) for k, v in arrays.items()}

    nc = _bacc.Bacc("TRN2", target_bir_lowering=False, num_devices=1)
    args = [nc.dram_tensor(k, v.shape, F32, kind="ExternalInput").ap() for k, v in arrays.items()]
    args.append(nc.dram_tensor("gate_scratch", (E, N), F32, kind="Internal").ap())
    args.append(nc.dram_tensor("out", (P, N), F32, kind="ExternalOutput").ap())
    build(nc, *args)
    r = _run(nc, [arrays], core_ids=[0])
    return np.ascontiguousarray(np.asarray(r.results[0]["out"]).T).reshape(IMAGES, SEQ, P)
```

```python
from contextlib import ExitStack

import numpy as np

import concourse.bass as bass
from concourse import mybir

F32 = mybir.dt.float32
F32R = mybir.dt.float32r
ACT = mybir.ActivationFunctionType
ALU = mybir.AluOpType
AX_X = mybir.AxisListType.X

P = 128
IMAGES, CHANNELS, IMG, PATCH = 32, 3, 112, 16
GRID = IMG // PATCH
SEQ = GRID * GRID
N = IMAGES * SEQ
KT = CHANNELS * PATCH * PATCH // P
DC, DS = 8, 4
HEADS, HD = 8, 16
HP = HEADS // 2
WINDOW = 5
E, FF, TOPK, SHARED = 64, 64, 6, 2
CAPACITY = max(1, int(N * TOPK * 2.0 / E))
EPS = 1e-5

CH = 4
CI = IMAGES // CH
CW = CI * SEQ
PW = 2 * SEQ
PAIRS = IMAGES // 2
TILES = CW // PW
QW = 64
XP = E // 2
GS = 4
LAG = 3
SENTINEL = -3.0e38

W_SPINCO, W_OUT, W_Q, W_K, W_V, W_O, W_ROUTER, W_EMBED = 0, 40, 168, 296, 424, 552, 1064, 1128
V0 = W_EMBED + 128
CO_AT = 32
(V_PATCH, V_EMBED, V_GAMMA, V_BETA, V_OUT, V_BQ, V_BK, V_OCR, V_BO, V_COORD, V_SPIN,
 V_BV) = range(V0, V0 + 12)
W_POS = V0 + 13
W_RBIAS = W_POS + SEQ
WCOLS = W_RBIAS + E
C_IDENT, C_CENTER, C_MEAN, C_ONES, C_BANDQ = 0, 128, 256, 384, 512
C_BANDK, C_PARITY, C_IMAGE, C_EPS = 640, 640 + CW, 642 + CW, 644 + CW
C_HP = C_EPS + 1
CCOLS = C_HP + HP


def build(nc, patches, w_patch, weights, consts, experts, gate_scratch, out):
    ctx = ExitStack()
    with ctx:
        def sb(name, shape, dt=F32):
            return ctx.enter_context(nc.sbuf_tensor(name, shape, dt))

        def sem(name):
            return ctx.enter_context(nc.semaphore(name))

        wpatch = sb("wpatch", [P, KT, P])
        wts = sb("wts", [P, WCOLS])
        cst = sb("cst", [P, CCOLS])
        pat = sb("pat", [P, KT, N])
        posb = sb("posb", [P, SEQ])
        x0 = sb("x0", [P, CH, CW])
        coords = sb("coords", [DC, CH, CW])
        spin2 = sb("spin2", [DS, CH, CW])
        xman = sb("xman", [P, CH, CW])
        xenh = sb("xenh", [P, CH, CW])
        sq = sb("sq", [P, CH, CW])
        xmk = sq
        logvar = sq
        rstd2 = sq
        rstd = sb("rstd", [P, CH, CW])
        ynorm = x0
        h1 = sb("h1", [P, N])
        xn = sb("xn", [P, N])
        btok = sb("btok", [P, 1])
        bproj = sb("bproj", [P, 1])
        bq1 = sb("bq1", [P, 1])
        qbias = sb("qbias", [P, 1])
        qT = xenh
        kT = xman
        bandq = sb("bandq", [PW, P], F32R)
        bandk = sb("bandk", [PW, CW], F32R)
        zeros = sb("zeros", [1, P], F32R)
        xpair = sb("xpair", [P, 2, PW])
        khead = sb("khead", [P, 2, 2, HP, SEQ])
        qdiag = sb("qdiag", [P, 2, 2, 2, QW])
        vdiag = sb("vdiag", [PW, 2, HP, 2, 2 * HD])
        smax = sb("smax", [P, 2, HEADS])
        sshift = sb("sshift", [P, 2, CW])
        probs = sb("probs", [P, 2, HP, 2, SEQ])
        ssum = sb("ssum", [P, 2, HEADS])
        rsum = sb("rsum", [P, 2, HEADS])
        probsT = sb("probsT", [PW, 2, HP * P])
        onorm = sb("onorm", [P, 2, 2 * HP * HD])
        oT = sb("oT", [P, 2, TILES, SEQ])
        h2 = sb("h2", [P, N])
        x2 = x0
        x2h = sb("x2h", [P, CH, CW], F32R)
        x2l = sb("x2l", [P, CH, CW], F32R)
        logits = sb("logits", [PW, CH, TILES, E + 2])
        top8 = sb("top8", [PW, CH, TILES, 8])
        top6 = sb("top6", [PW, CH, TILES, 8])
        marked = sb("marked", [PW, CH, TILES, E + 2])
        lboth = sb("lboth", [PW, CH, 2, TILES, E])
        lexp, lsel = lboth[:, :, 0, :, :], lboth[:, :, 1, :, :]
        lsum = sb("lsum", [PW, CH, 4, TILES])
        gsel = sb("gsel", [PW, CH, TILES, 2 * E])
        gT = pat[0:E, 4, :].rearrange("p (a b) -> p a b", a=CH)
        rank = pat[0:E, 5, :].rearrange("p (a b) -> p a b", a=CH)
        ones_row = sb("ones_row", [E, CW])
        gateT = gT
        wraw = sb("wraw", [P, 2, 3 * P])
        wh = sb("wh", [P, 2, 3 * P], F32R)
        wl = sb("wl", [P, 2, 3 * P], F32R)
        half = sb("half", [P, CW])
        gbc = pat[:, 0:GS, :]
        act_g = sb("act_g", [P, 2, CW])
        prod = sb("prod", [P, 2, CW])
        hid = sb("hid", [P, 2, CW])
        hidh = sb("hidh", [P, CH, CW], F32R)
        hidl = sb("hidl", [P, CH, CW], F32R)
        result = xman

        bank = [ctx.enter_context(nc.psum_tensor(f"bank{i}", [P, 512], F32)) for i in range(8)]
        bA, bB = (bank[2], bank[1], bank[5], bank[0]), (bank[3], bank[4], bank[6], bank[7])
        b_cen, b_v, b_s, b_pT, b_o, b_oT, b_proj = bank[0], bank[1], bank[2:4], bank[4], bank[5], bank[6], bank[7]
        b_var = b_proj
        b_logits, b_gT = (b_s[0], b_v, b_v, b_v), (b_o, b_oT)
        b_gu, b_sum = (bank[2:4], bank[0:2]), bank[4:8]

        s_wpatch, s_weights, s_consts = sem("wpatch_in"), sem("weights_in"), sem("consts_in")
        s_pat = [sem(f"patches_in{c}") for c in range(CH)]
        s_pat_rest = sem("patches_in0_rest")
        posb_ready, biasmm_ready, bias_ready = sem("posb_ready"), sem("biasmm_ready"), sem("bias_ready")
        half_ready = sem("half_ready")
        bq1_ready, qbias_ready, band_ready = sem("bq1_ready"), sem("qbias_ready"), sem("band_ready")
        pads_ready, zeros_ready = sem("pads_ready"), sem("zeros_ready")
        x0_mm, x0_ready = sem("x0_mm"), sem("x0_ready")
        cs_mm, spinco_ready = sem("cs_mm"), sem("spinco_ready")
        man_mm, xman_ready, xmk_ready, xenh_ready = sem("man_mm"), sem("xman_ready"), sem("xmk_ready"), sem("xenh_ready")
        cen_mm = [sem(f"cen_mm{n}") for n in range(3)]
        sq_ready = [sem(f"sq_ready{n}") for n in range(3)]
        var_mm = [sem(f"var_mm{n}") for n in range(3)]
        logvar_ready = [sem(f"logvar_ready{n}") for n in range(3)]
        rstd2_ready = [sem(f"rstd2_ready{n}") for n in range(3)]
        refine_step = [sem(f"refine_step{n}") for n in range(3)]
        rstd_ready = [sem(f"rstd_ready{n}") for n in range(3)]
        norm_ready = [sem(f"norm_ready{n}") for n in range(3)]
        qk_mm, q_ready, k_ready = sem("qk_mm"), sem("q_ready"), sem("k_ready")
        h1_mm, h1_ready = sem("h1_mm"), sem("h1_ready")
        xpair_ready, qdiag_ready, khead_ready, v_mm, vdiag_ready = (
            sem("xpair_ready"), sem("qdiag_ready"), sem("khead_ready"), sem("v_mm"), sem("vdiag_ready"))
        scores_mm, smax_ready, sshift_ready, probs_ready, ssum_ready, rsum_ready = (
            sem("scores_mm"), sem("smax_ready"), sem("sshift_ready"), sem("probs_ready"), sem("ssum_ready"), sem("rsum_ready"))
        pT_mm, probsT_ready, o_mm, onorm_ready, oT_mm, oT_ready, proj_mm, h2_ready = (
            sem("pT_mm"), sem("probsT_ready"), sem("o_mm"), sem("onorm_ready"), sem("oT_mm"), sem("oT_ready"), sem("proj_mm"), sem("h2_ready"))
        x2h_ready, x2l_ready = sem("x2h_ready"), sem("x2l_ready")
        logits_mm, logits_ready = sem("logits_mm"), sem("logits_ready")
        top8_ready, lshift_ready, top6_ready, marked_ready, chosen_ready, lexp_ready, lsel_ready, lsum_step = (
            sem("top8_ready"), sem("lshift_ready"), sem("top6_ready"), sem("marked_ready"), sem("chosen_ready"), sem("lexp_ready"),
            sem("lsel_ready"), sem("lsum_step"))
        gsel_ready, gT_mm, gT_ready, rank_ready, gateT_ready = (
            sem("gsel_ready"), sem("gT_mm"), sem("gT_ready"), sem("rank_ready"), sem("gateT_ready"))
        gate_stored = [sem(f"gate_stored{c}") for c in range(CH)]
        s_wraw = [sem(f"expert_in{s}") for s in range(2)]
        s_gfirst = [sem(f"first_gates_in{c}") for c in range(CH)]
        s_gbc = [sem(f"gates_in{s}") for s in range(GS)]
        wgu_high, wgu_low, wd_high, wd_low = sem("wgu_high"), sem("wgu_low"), sem("wd_high"), sem("wd_low")
        hidh_ready, hidl_ready = sem("hidh_ready"), sem("hidl_ready")
        gu_mm, actg_ready, prod_ready, hid_ready, down_mm = sem("gu_mm"), sem("actg_ready"), sem("prod_ready"), sem("hid_ready"), sem("down_mm")
        result_ready, s_out = sem("result_ready"), sem("out_stored")

        def w(a, n, rows=P):
            return wts[0:rows, a:a + n]

        def c_(a, n, rows=P):
            return cst[0:rows, a:a + n]

        ident = c_(C_IDENT, P)
        x2flat, x2hflat, x2lflat = (a[:, :, :].rearrange("p a b -> p (a b)") for a in (x2, x2h, x2l))
        qflat, kflat = qT[:, :, :].rearrange("p a b -> p (a b)"), kT[:, :, :].rearrange("p a b -> p (a b)")
        chunk = [slice(c * CW, (c + 1) * CW) for c in range(CH)]

        def bcast(ap, axis, count):
            ap = ap.unsqueeze(axis)
            shape = list(ap.shape)
            shape[axis] = count
            return ap.to_broadcast(shape)

        TOK_STAGES = 11
        START = []
        for n in range(TOK_STAGES + CH - 1):
            wave = [(n - c, c) for c in reversed(range(CH)) if 0 <= n - c < TOK_STAGES]
            START += wave[1:] + wave[:1] if n <= 1 else wave
            START += {TOK_STAGES: [("fetch", 0), ("fetch", 1)], TOK_STAGES + 1: [("attend", 0)], TOK_STAGES + 2: [("attend", 1)]}.get(n, [])

        def start(stages, **turns):
            parts = dict(enumerate(stages), **turns)
            for name, c in START:
                if parts.get(name):
                    parts[name](c)

        FIRST = TILES + 1
        LOOPS = CH - 2
        TAIL = (("attend", 13), ("upper", 0), ("fetch", 15), ("attend", 14), ("upper", 1), ("project", 2), ("attend", 15),
                ("variance", 2), ("logits", 0), ("attend", 16), ("norm", 2), ("upper", 2), ("attend", 17), ("choose", 0),
                ("gate_up", 0), ("attend", 18), ("project", 3), ("centre", 3), ("choose", 1), ("scale", 0), ("logits", 2),
                ("variance", 3), ("sum", 0), ("gates", 0), ("scale", 1), ("norm", 3), ("upper", 3), ("gates", 1), ("logits", 3),
                ("choose", 2), ("admit", 0), ("choose", 3), ("gate_up", 1), ("scale", 2), ("scale", 3), ("hidden", 0), ("gates", 2),
                ("admit", 1), ("hidden", 1), ("gates", 3), ("gate_up", 2), ("admit", 2), ("hidden", 2), ("gate_up", 3), ("admit", 3),
                ("sum", 3), ("sum", 1), ("sum", 2), ("hidden", 3))

        def tail(stages):
            for name, c in TAIL:
                if name in stages:
                    stages[name](c)

        block = ctx.enter_context(nc.Block())

        @block.sync
        def _(sp):
            sp.dma_start(wpatch[:, :, :], w_patch).then_inc(s_wpatch, 16)
            for h in range(2):
                k = slice(h * KT // 2, (h + 1) * KT // 2)
                sp.dma_start(pat[:, k, chunk[0]], patches[:, k, chunk[0]]).then_inc((s_pat[0], s_pat_rest)[h], 16)
            sp.dma_start(wts[:, :], weights).then_inc(s_weights, 16)
            sp.dma_start(cst[:, :], consts).then_inc(s_consts, 16)
            for c in range(1, CH):
                sp.dma_start(pat[:, :, chunk[c]], patches[:, :, chunk[c]]).then_inc(s_pat[c], 16)
            for s in range(2):
                sp.dma_start(wraw[:, s, :], experts[s]).then_inc(s_wraw[s], 16)

            def load_gates(j, s):
                sp.dma_start(gbc[:, s, :], bcast(gate_scratch[bass.ds(2 * j, 2), :], 1, FF)).then_inc(s_gbc[s], 16)

            def refill_weights(p, s):
                sp.wait_ge(wgu_low, p - 1)
                sp.wait_ge(wd_low, p - 1)
                sp.dma_start(wraw[:, s, :], experts[bass.ds(p, 1), :, :].rearrange("a p n -> p (a n)")).then_inc(s_wraw[s], 16)

            def refill_gates(j, s):
                sp.wait_ge(hid_ready, CH * (j - GS + 2))
                load_gates(j, s)

            refill_weights(2, 0)
            refill_weights(3, 1)

            def store_gates(c):
                sp.wait_ge(gateT_ready, c + 1)
                sp.dma_start(gate_scratch[:, chunk[c]], gateT[:, c, :]).then_inc(gate_stored[c], 16)

            def load_first_gates(c):
                sp.wait_ge(gate_stored[c], 16)
                for j in range(2):
                    sp.dma_start(gbc[:, j, chunk[c]], bcast(gate_scratch[2 * j:2 * j + 2, chunk[c]], 1, FF)).then_inc(s_gfirst[c], 16)

            store_gates(0)
            for c in range(1, CH):
                store_gates(c)
                load_first_gates(c - 1)
            load_first_gates(CH - 1)
            for j in range(2, GS):
                load_gates(j, j)
            with sp.Fori(0, XP // GS - 1) as r:
                for v in range(GS):
                    refill_weights(GS * r + (GS + v), v % 2)
                    refill_gates(GS * r + (GS + v), v)
            refill_weights(XP, 0)
            for c in range(CH):
                sp.wait_ge(result_ready, c + 1)
                sp.dma_start(out[:, chunk[c]], result[:, c, :]).then_inc(s_out, 16)
            sp.wait_ge(s_out, 16 * CH)

        @block.tensor
        def _(pe):
            pe.wait_ge(s_wpatch, 16)

            def patch_product(c):
                pe.wait_ge(s_pat[c], 16)
                for k in range(KT):
                    if c == 0 and k == KT // 2:
                        pe.wait_ge(s_pat_rest, 16)
                    last = pe.matmul(bA[c][:, 0:CW], wpatch[:, k, :], pat[:, k, chunk[c]], start=(k == 0), stop=(k == KT - 1))
                last.then_inc(x0_mm, 1)

            def folded_biases():
                pe.wait_ge(s_weights, 16)
                pe.matmul(bB[3][:, 0:1], w(W_OUT, P), w(V_BETA, 1), start=True, stop=True)
                for t in range(2):
                    last = pe.matmul(bB[3][:, 1:2], w(W_O + t * P, P), w(V_BV + t, 1), start=(t == 0), stop=(t == 1))
                last.then_inc(biasmm_ready, 1)

            def spinors_coordinates(c):
                if c == 0:
                    folded_biases()
                    pe.wait_ge(s_consts, 16)
                if c == 3:
                    pe.wait_ge(bias_ready, 2)
                pe.wait_ge(x0_ready, c + 1)
                pe.matmul(bB[c][0:CO_AT + DC, 0:CW], w(W_SPINCO, CO_AT + DC), x0[:, c, :], start=True, stop=True).then_inc(cs_mm, 1)

            def manifold(c):
                pe.wait_ge(spinco_ready, c + 1)
                pe.matmul(bA[c][:, 0:CW], w(W_EMBED, P, DC), coords[:, c, :], start=True, stop=True)
                pe.matmul(bB[c][:, 0:CW], c_(C_ONES, P, DS), spin2[:, c, :], start=True, stop=True).then_inc(man_mm, 1)

            def centre(n, c, src, ready):
                pe.wait_ge(ready, c + 1)
                pe.matmul(bA[c][:, 0:CW], c_(C_CENTER, P), src, start=True, stop=True).then_inc(cen_mm[n], 1)

            def variance(n, c):
                pe.wait_ge(sq_ready[n], c + 1)
                pe.matmul(bB[c][:, 0:CW], c_(C_MEAN, P), sq[:, c, :], start=True, stop=True).then_inc(var_mm[n], 1)

            def tokenizer_out(c):
                pe.wait_ge(norm_ready[0], c + 1)
                pe.matmul(bB[c][:, 0:CW], w(W_OUT, P), ynorm[:, c, :], start=True, stop=True).then_inc(h1_mm, 1)

            def queries_keys(c):
                pe.wait_ge(norm_ready[1], c + 1)
                pe.matmul(bA[c][:, 0:CW], w(W_Q, P), xn[:, chunk[c]], start=True, stop=True)
                pe.matmul(bB[c][:, 0:CW], w(W_K, P), xn[:, chunk[c]], start=True, stop=True).then_inc(qk_mm, 1)

            stages = (patch_product, spinors_coordinates, manifold, lambda c: centre(0, c, xenh[:, c, :], xenh_ready),
                      lambda c: variance(0, c), None, tokenizer_out, lambda c: centre(1, c, h1[:, chunk[c]], h1_ready),
                      lambda c: variance(1, c), None, queries_keys)

            def project_v(j, s, n):
                pe.wait_ge(xpair_ready, j + 1)
                if n >= 1:
                    pe.wait_ge(vdiag_ready, j)
                pe.matmul(b_v[0:PW, 0:P], xpair[:, s, :], w(W_V, P), start=True, stop=True).then_inc(v_mm, 1)

            def scores(j, s, n):
                pe.wait_ge(qdiag_ready, j + 1)
                pe.wait_ge(khead_ready, j + 1)
                if n >= 2:
                    pe.wait_ge(sshift_ready, j - 1)
                pe.matmul(b_s[s][:, 0:CW], bandq[:, :], bandk[:, :], start=True, stop=False)
                for m in range(2):
                    last = pe.matmul(b_s[s][:, 0:CW].rearrange("p (h m k) -> p h m k", h=HP, m=2)[:, :, m, :],
                                     qdiag[:, s, m, :, :].rearrange("p a b -> p (a b)"), khead[:, s, m, :, :], start=False, stop=(m == 1))
                last.then_inc(scores_mm, 1)

            def transpose_probs(j, s, n):
                pe.wait_ge(probs_ready, j + 1)
                if n >= 1:
                    pe.wait_ge(probsT_ready, j)
                for hp in range(HP):
                    last = pe.transpose(b_pT[0:PW, hp * P:(hp + 1) * P], probs[:, s, hp, :, :].rearrange("p a b -> p (a b)"), ident)
                last.then_inc(pT_mm, 1)

            def weigh_values(j, s, n):
                pe.wait_ge(probsT_ready, j + 1)
                pe.wait_ge(vdiag_ready, j + 1)
                if n >= 1:
                    pe.wait_ge(onorm_ready, j)
                for hp in range(HP):
                    last = pe.matmul(b_o[:, hp * 64:(hp + 1) * 64], probsT[:, s, hp * P:(hp + 1) * P],
                                     vdiag[:, s, hp, :, :].rearrange("p a b -> p (a b)"), start=True, stop=True)
                last.then_inc(o_mm, 1)

            def transpose_out(j, s, n):
                pe.wait_ge(onorm_ready, j + 1)
                if n >= 1:
                    pe.wait_ge(oT_ready, j)
                pe.transpose(b_oT[:, 0:P], onorm[:, s, :], ident).then_inc(oT_mm, 1)

            def project_out(c):
                pe.wait_ge(oT_ready, TILES * (c + 1))
                for m in range(2):
                    for t in range(2):
                        last = pe.matmul(b_proj[:, 0:CW].rearrange("p (u m q) -> p u m q", u=TILES, m=2)[:, :, m, :], w(W_O + (2 * m + t) * P, P),
                                         oT[:, t, :, :], start=(t == 0), stop=(t == 1))
                last.then_inc(proj_mm, 1)

            def attend(j, n, between=None):
                if 2 <= n <= PAIRS + 1:
                    transpose_probs(j - 2, n % 2, n - 2)
                if n < PAIRS:
                    scores(j, n % 2, n)
                if between:
                    between()
                if 1 <= n <= PAIRS:
                    project_v(j - 1, (n - 1) % 2, n - 1)
                if n >= 3:
                    transpose_out(j - 3, (n - 1) % 2, n - 3)
                if 2 <= n <= PAIRS + 1:
                    weigh_values(j - 2, n % 2, n - 2)

            def centre_out(c):
                pe.wait_ge(h2_ready, c + 1)
                pe.matmul(b_cen[:, 0:CW], c_(C_CENTER, P), h2[:, bass.ds(c * CW, CW)], start=True, stop=True).then_inc(cen_mm[2], 1)

            def variance_out(c):
                pe.wait_ge(sq_ready[2], c + 1)
                pe.matmul(b_var[:, 0:CW], c_(C_MEAN, P), sq[:, 0, :], start=True, stop=True).then_inc(var_mm[2], 1)

            def first_turn(n):
                if n == 0:
                    pe.wait_ge(band_ready, 2)
                else:
                    pe.wait_ge(q_ready, 2)
                    pe.wait_ge(k_ready, 2)
                attend(n, n)

            start(stages, attend=first_turn)
            pe.wait_ge(q_ready, CH)
            pe.wait_ge(k_ready, CH)
            for n in range(2, FIRST):
                attend(n, n)
            with pe.Fori(0, LOOPS) as r:
                for u in range(TILES):
                    attend(TILES * r + (FIRST + u), FIRST + u, (lambda: centre_out(r)) if u == 2 else None)
                    if u == 1:
                        project_out(r)
                    if u == 2:
                        variance_out(r)

            def router_logits(c):
                pe.wait_ge(norm_ready[2], c + 1)
                if c == 0:
                    pe.wait_ge(sshift_ready, PAIRS - 1)
                elif c == 1:
                    pe.wait_ge(vdiag_ready, PAIRS)
                else:
                    pe.wait_ge(logits_ready, c)
                pe.matmul(b_logits[c][0:PW, 0:TILES * E].rearrange("p (a b) -> p a b", a=TILES), c_(C_ONES, PW, 1), bcast(w(W_RBIAS, E, 1), 1, TILES),
                          start=True, stop=False)
                for t in range(TILES):
                    last = pe.matmul(b_logits[c][0:PW, t * E:(t + 1) * E], x2[:, c, t * PW:(t + 1) * PW], w(W_ROUTER, E),
                                     start=False, stop=(t == TILES - 1))
                last.then_inc(logits_mm, 1)

            def gates_by_expert(c):
                pe.wait_ge(gsel_ready, c + 1)
                if c < 2:
                    pe.wait_ge(oT_ready, PAIRS)
                else:
                    pe.wait_ge(gT_ready, c - 1)
                    pe.wait_ge(rank_ready, c - 1)
                for t in range(TILES):
                    last = pe.transpose(b_gT[c % 2][:, t * PW:(t + 1) * PW], gsel[:, c, t, :], c_(C_IDENT, PW, PW))
                last.then_inc(gT_mm, 1)

            def gate_up(k, p, c, hs, first=False):
                g, u = b_gu[c % 2]
                if c == 0:
                    pe.wait_ge(wgu_low, p + 1)
                if not first:
                    pe.wait_ge(prod_ready, k - 1)
                for b, a in ((g, 0), (u, P)):
                    pe.matmul(b[:, 0:CW], wh[:, hs, a:a + P], x2h[:, c, :], start=True, stop=False)
                    pe.matmul(b[:, 0:CW], wh[:, hs, a:a + P], x2l[:, c, :], start=False, stop=False)
                    last = pe.matmul(b[:, 0:CW], wl[:, hs, a:a + P], x2h[:, c, :], start=False, stop=True)
                last.then_inc(gu_mm, 1)

            def down(k, p, c, hs):
                if c == 0:
                    pe.wait_ge(wd_low, p + 1)
                pe.wait_ge(hidl_ready, k + 1)
                a = 2 * P
                for x, y in ((wh, hidh), (wh, hidl), (wl, hidh)):
                    last = pe.matmul(b_sum[c][:, 0:CW], x[:, hs, a:a + P], y[:, c, :], start=False, stop=True, skip_group_check=True)
                last.then_inc(down_mm, 1)

            def shared_gate_up(c):
                if c == 0:
                    pe.wait_ge(logits_ready, 1)
                    pe.wait_ge(sshift_ready, PAIRS)
                if c == 1:
                    pe.wait_ge(logits_ready, CH)
                pe.wait_ge(x2l_ready, c + 1)
                gate_up(c, 0, c, 0, first=(c < 2))

            def start_sum(c):
                if c == 0:
                    pe.wait_ge(zeros_ready, 1)
                    pe.wait_ge(probsT_ready, PAIRS)
                elif c == CH - 1:
                    pe.wait_ge(norm_ready[2], CH)
                else:
                    pe.wait_ge(gT_ready, CH - 2 + c)
                    pe.wait_ge(rank_ready, CH - 2 + c)
                pe.matmul(b_sum[c][:, 0:CW], zeros[:, :], bandk[0:1, :], start=True, stop=True).then_inc(down_mm, 1)

            between = {15: lambda: centre_out(2), 17: lambda: router_logits(1)}
            tail({"logits": router_logits, "attend": lambda n: attend(n, n, between.get(n)),
                  "project": project_out, "centre": centre_out, "variance": variance_out, "gates": gates_by_expert,
                  "gate_up": shared_gate_up, "sum": start_sum})

            for c in range(CH - LAG):
                down(c, 0, c, 0)
            with pe.Fori(0, XP // 2) as r:
                for v in range(2):
                    p = 2 * r + (v + 1)
                    for c in range(CH):
                        gate_up(CH * p + c, p, c, (v + 1) % 2)
                        back = c - LAG
                        if back < 0:
                            down(CH * p + back, p - 1, back + CH, v)
                        else:
                            down(CH * p + back, p, back, (v + 1) % 2)
            for c in range(CH - LAG, CH):
                down(CH * XP + c, XP, c, XP % 2)

        @block.scalar
        def _(act):
            act.preload_act_table_set("natural_log_exp_and_others")
            act.wait_ge(s_weights, 16)
            act.wait_ge(s_consts, 16)

            def take_spinco(c):
                act.wait_ge(cs_mm, c + 1)
                act.activation(spin2[:, c, :], bB[c][0:DS, 0:CW], ACT.Square, bias=w(V_SPIN, 1, DS))
                act.activation(coords[:, c, :], bB[c][CO_AT:CO_AT + DC, 0:CW], ACT.Identity, bias=w(V_COORD, 1, DC)).then_inc(spinco_ready, 1)

            def take_manifold(c):
                act.wait_ge(man_mm, c + 1)
                act.activation(xman[:, c, :], bA[c][:, 0:CW], ACT.Identity, bias=w(V_EMBED, 1)).then_inc(xman_ready, 1)

            def squares(n, c):
                act.wait_ge(cen_mm[n], c + 1)
                act.activation(sq[:, c, :], bA[c][:, 0:CW], ACT.Square).then_inc(sq_ready[n], 1)

            def deviation(n, c):
                act.wait_ge(var_mm[n], c + 1)
                act.activation(logvar[:, c, :], bB[c][:, 0:CW], ACT.Ln, bias=c_(C_EPS, 1), scale=2.0).then_inc(logvar_ready[n], 1)
                act.wait_ge(logvar_ready[n], c + 1)
                act.activation(rstd[:, c, :], logvar[:, c, :], ACT.Exp, scale=-0.5).then_inc(rstd_ready[n], 1)

            def take_h1(c):
                if c == 0:
                    act.wait_ge(bias_ready, 2)
                act.wait_ge(h1_mm, c + 1)
                act.activation(h1[:, chunk[c]], bB[c][:, 0:CW], ACT.Identity, bias=btok[:, :]).then_inc(h1_ready, 1)

            def take_q(c):
                if c == 0:
                    act.wait_ge(qbias_ready, 1)
                act.wait_ge(qk_mm, c + 1)
                act.activation(qT[:, c, :], bA[c][:, 0:CW], ACT.Identity, bias=qbias[:, :], scale=1.0 / HD ** 0.5).then_inc(q_ready, 1)

            stages = (None, take_spinco, take_manifold, lambda c: squares(0, c), lambda c: deviation(0, c), None, take_h1,
                      lambda c: squares(1, c), lambda c: deviation(1, c), None, take_q)

            def split_gate_up(p, hs, first=False):
                act.wait_ge(s_wraw[hs], 8 * (p - hs) + 16)
                if not first:
                    act.wait_ge(gu_mm, CH * (p - 1))
                act.activation(wh[:, hs, 0:2 * P], wraw[:, hs, 0:2 * P], ACT.Copy).then_inc(wgu_high, 1)

            def split_down(p, hs, first=False):
                if not first:
                    act.wait_ge(down_mm, CH * p)
                act.activation(wh[:, hs, 2 * P:3 * P], wraw[:, hs, 2 * P:3 * P], ACT.Copy).then_inc(wd_high, 1)

            def take_probsT(j, s, n):
                act.wait_ge(pT_mm, j + 1)
                if n >= 2:
                    act.wait_ge(o_mm, j - 1)
                act.activation(probsT[:, s, :], b_pT[0:PW, :], ACT.Identity).then_inc(probsT_ready, 1)

            def exponentials(j, s, n):
                act.wait_ge(sshift_ready, j + 1)
                if n >= 2:
                    act.wait_ge(pT_mm, j - 1)
                    act.wait_ge(ssum_ready, j - 1)
                act.activation(probs[:, s, :, :, :].rearrange("p a b c -> p (a b c)"), sshift[:, s, :], ACT.Exp).then_inc(probs_ready, 1)

            def take_v(j, s, n):
                act.wait_ge(v_mm, j + 1)
                if n >= 2:
                    act.wait_ge(o_mm, j - 1)
                for t in range(2):
                    last = act.activation(vdiag[:, s, :, t, :], b_v[0:PW, 0:P].rearrange("p (a b) -> p a b", a=HP), ACT.Copy,
                                          scale=c_(C_IMAGE + t, 1, PW))
                last.then_inc(vdiag_ready, 1)

            def take_oT(j, n):
                act.wait_ge(oT_mm, j + 1)
                act.activation(oT[:, :, n % TILES, :], b_oT[:, 0:P].rearrange("p (t q) -> p t q", t=2)[:, :, 0:SEQ],
                               ACT.Identity).then_inc(oT_ready, 1)

            def attend(j, n, between=None):
                if 2 <= n <= PAIRS + 1:
                    take_probsT(j - 2, n % 2, n - 2)
                if 1 <= n <= PAIRS:
                    take_v(j - 1, (n - 1) % 2, n - 1)
                if between:
                    between()
                if n >= 3:
                    take_oT(j - 3, n - 3)
                if n < PAIRS:
                    exponentials(j, n % 2, n)

            def squares_out(c):
                act.wait_ge(cen_mm[2], c + 1)
                act.activation(sq[:, 0, :], b_cen[:, 0:CW], ACT.Square).then_inc(sq_ready[2], 1)

            def deviation_out(c):
                act.wait_ge(var_mm[2], c + 1)
                act.activation(logvar[:, 0, :], b_var[:, 0:CW], ACT.Ln, bias=c_(C_EPS, 1), scale=2.0).then_inc(logvar_ready[2], 1)
                act.wait_ge(logvar_ready[2], c + 1)
                act.activation(rstd[:, 0, :], logvar[:, 0, :], ACT.Exp, scale=-0.5).then_inc(rstd_ready[2], 1)
                act.wait_ge(rstd_ready[2], c + 1)
                act.activation(rstd2[:, 0, :], rstd[:, 0, :], ACT.Square).then_inc(rstd2_ready[2], 1)

            def upper_x(c):
                at = bass.ds(c * CW, CW)
                act.wait_ge(norm_ready[2], c + 1)
                act.activation(x2hflat[:, at], x2flat[:, at], ACT.Copy).then_inc(x2h_ready, 1)

            start(stages, attend=lambda n: attend(n, n))
            for p in range(2):
                split_gate_up(p, p, True)
                split_down(p, p, True)
            for n in range(2, FIRST):
                attend(n, n)
            with act.Fori(0, LOOPS) as r:
                for u in range(TILES):
                    if u == 2:
                        act.wait_ge(proj_mm, r + 1)
                    attend(TILES * r + (FIRST + u), FIRST + u, (lambda: squares_out(r)) if u == 2 else None)
                    if u == 2:
                        deviation_out(r)

            def take_logits(c):
                act.wait_ge(logits_mm, c + 1)
                act.activation(logits[:, c, :, 0:E], b_logits[c][0:PW, 0:TILES * E].rearrange("p (a b) -> p a b", a=TILES),
                               ACT.Identity).then_inc(logits_ready, 1)

            def exponentials_logits(c):
                act.wait_ge(lshift_ready, c + 1)
                act.activation(lexp[:, c, :, :], lsel[:, c, :, :], ACT.Exp).then_inc(lexp_ready, 1)

            def take_gT(c):
                act.wait_ge(gT_mm, c + 1)
                act.activation(gT[:, c, :], b_gT[c % 2][E:2 * E, 0:CW], ACT.Identity).then_inc(gT_ready, 1)

            def silu(k, c, first=False):
                act.wait_ge(gu_mm, k + 1)
                if not first:
                    act.wait_ge(prod_ready, k - 1)
                act.activation(act_g[:, c % 2, :], b_gu[c % 2][0][:, 0:CW], ACT.Silu).then_inc(actg_ready, 1)

            def high(k, c, first=False):
                act.wait_ge(hid_ready, k + 1)
                if not first:
                    act.wait_ge(down_mm, k + 1)
                act.activation(hidh[:, c, :], hid[:, c % 2, :], ACT.Copy).then_inc(hidh_ready, 1)

            def shared_hidden(c):
                silu(c, c, c < 2)
                if c:
                    high(c - 1, c - 1, True)

            def last_turns(n):
                if n == 15:
                    act.wait_ge(proj_mm, CH - 1)
                attend(n, n, {15: lambda: squares_out(2), 17: lambda: take_logits(1)}.get(n))

            tail({"logits": take_logits, "attend": last_turns, "centre": squares_out, "choose": exponentials_logits,
                  "variance": deviation_out, "upper": upper_x, "gates": take_gT,
                  "hidden": shared_hidden})

            def expert_turns(p, hs, last=False):
                for c in range(CH):
                    silu(CH * p + c, c)
                    high(CH * p + (c - 1), (c - 1) % CH)
                    if not last:
                        if c == 1:
                            split_gate_up(p + 1, 1 - hs)
                        if c == 3:
                            split_down(p + 1, 1 - hs)

            with act.Fori(0, XP // 2 - 1) as r:
                for v in range(2):
                    expert_turns(2 * r + (v + 1), 1 - v)
            expert_turns(XP - 1, 1)
            expert_turns(XP, 0, last=True)
            high(CH * XP + CH - 1, CH - 1)

        @block.vector
        def _(dve):
            dve.wait_ge(s_weights, 16)
            dve.tensor_scalar(posb[:, :], w(W_POS, SEQ), w(V_PATCH, 1), None, ALU.add).then_inc(posb_ready, 1)
            dve.tensor_tensor(bq1[:, :], w(V_BQ, 1), w(V_OCR, 1), ALU.add).then_inc(bq1_ready, 1)
            dve.wait_ge(s_consts, 16)
            dve.tensor_copy(bandq[:, :], c_(C_BANDQ, P, PW)).then_inc(band_ready, 1)
            dve.tensor_scalar(zeros[:, :], c_(C_ONES, P, 1), 0.0, None, ALU.mult).then_inc(zeros_ready, 1)
            dve.tensor_copy(bandk[:, :], c_(C_BANDK, CW, PW)).then_inc(band_ready, 1)
            dve.wait_ge(bq1_ready, 1)
            dve.tensor_scalar(qbias[:, :], bq1[:, :], 1.0 / HD ** 0.5, None, ALU.mult).then_inc(qbias_ready, 1)

            def embed(c):
                if c == 0:
                    dve.wait_ge(posb_ready, 1)
                dve.wait_ge(x0_mm, c + 1)
                dve.tensor_tensor(x0[:, c, :].rearrange("p (a b) -> p a b", a=CI), bA[c][:, 0:CW].rearrange("p (a b) -> p a b", a=CI),
                                  bcast(posb[:, :], 1, CI), ALU.add).then_inc(x0_ready, 1)
                if c == 0:
                    dve.wait_ge(biasmm_ready, 1)
                    dve.tensor_tensor(btok[:, :], bB[3][:, 0:1], w(V_OUT, 1), ALU.add).then_inc(bias_ready, 1)
                    dve.tensor_tensor(bproj[:, :], bB[3][:, 1:2], w(V_BO, 1), ALU.add).then_inc(bias_ready, 1)

            def enhance(c):
                dve.wait_ge(xman_ready, c + 1)
                dve.tensor_tensor(xmk[:, c, :], bB[c][:, 0:CW], xman[:, c, :], ALU.mult).then_inc(xmk_ready, 1)
                dve.wait_ge(xmk_ready, c + 1)
                dve.tensor_tensor(xenh[:, c, :], xmk[:, c, :], x0[:, c, :], ALU.add).then_inc(xenh_ready, 1)

            def norm(n, c, out, gamma=None):
                dve.wait_ge(rstd2_ready[n], c + 1)
                dve.scalar_tensor_tensor(rstd2[:, c, :], bB[c][:, 0:CW], EPS / 2, rstd2[:, c, :], ALU.add, ALU.mult).then_inc(refine_step[n], 1)
                dve.wait_ge(refine_step[n], 2 * c + 1)
                dve.scalar_tensor_tensor(rstd[:, c, :], rstd2[:, c, :], -1.5, rstd[:, c, :], ALU.add, ALU.mult).then_inc(refine_step[n], 1)
                dve.wait_ge(refine_step[n], 2 * c + 2)
                if gamma is None:
                    dve.tensor_tensor(out, bA[c][:, 0:CW], rstd[:, c, :], ALU.mult).then_inc(norm_ready[n], 1)
                else:
                    dve.scalar_tensor_tensor(out, bA[c][:, 0:CW], gamma, rstd[:, c, :], ALU.mult, ALU.mult).then_inc(norm_ready[n], 1)

            def take_k(c):
                dve.wait_ge(qk_mm, c + 1)
                dve.tensor_scalar(kT[:, c, :], bB[c][:, 0:CW], w(V_BK, 1), None, ALU.add).then_inc(k_ready, 1)

            stages = (embed, None, enhance, None, None, lambda c: norm(0, c, ynorm[:, c, :], w(V_GAMMA, 1)), None, None, None,
                      lambda c: norm(1, c, xn[:, chunk[c]]), take_k)

            def shift(j, s, n):
                dve.wait_ge(scores_mm, j + 1)
                sc = b_s[s][:, 0:CW].rearrange("p (a b) -> p a b", a=HEADS)
                dve.tensor_reduce(smax[:, s, :], sc, AX_X, ALU.max).then_inc(smax_ready, 1)
                dve.wait_ge(smax_ready, j + 1)
                if n >= 2:
                    dve.wait_ge(probs_ready, j - 1)
                dve.tensor_tensor(sshift[:, s, :].rearrange("p (a b) -> p a b", a=HEADS), sc, bcast(smax[:, s, :], 2, SEQ),
                                  ALU.subtract).then_inc(sshift_ready, 1)

            def sums(j, s):
                dve.wait_ge(probs_ready, j + 1)
                dve.tensor_reduce(ssum[:, s, :], probs[:, s, :, :, :].rearrange("p a b c -> p (a b) c"), AX_X, ALU.add).then_inc(ssum_ready, 1)
                dve.wait_ge(ssum_ready, j + 1)
                dve.reciprocal(rsum[:, s, :], ssum[:, s, :]).then_inc(rsum_ready, 1)

            def take_o(j, s, n):
                dve.wait_ge(o_mm, j + 1)
                dve.wait_ge(rsum_ready, j + 1)
                if n >= 2:
                    dve.wait_ge(oT_mm, j - 1)
                for t in range(2):
                    rows = slice(QW * t, QW * (t + 1))
                    o = b_o[rows, 0:4 * HP * HD].rearrange("p (h m t d) -> p h m t d", h=HP, m=2, t=2)[:, :, :, t, :]
                    r = rsum[rows, s, :].rearrange("p (h m) -> p h m", m=2)
                    last = dve.tensor_tensor(onorm[rows, s, :].rearrange("p (m h d) -> p h m d", m=2, h=HP), o, bcast(r, 3, HD), ALU.mult)
                last.then_inc(onorm_ready, 1)

            def residual(c):
                dve.wait_ge(proj_mm, c + 1)
                at = bass.ds(c * CW, CW)
                dve.scalar_tensor_tensor(h2[:, at], b_proj[:, 0:CW], bproj[:, :], h1[:, at], ALU.add, ALU.add).then_inc(h2_ready, 1)

            def attend(j, n):
                if n >= 3:
                    take_o(j - 3, (n - 1) % 2, n - 3)
                if 1 <= n <= PAIRS:
                    sums(j - 1, (n - 1) % 2)
                if n < PAIRS:
                    shift(j, n % 2, n)

            def norm_out(c):
                dve.wait_ge(rstd2_ready[2], c + 1)
                dve.scalar_tensor_tensor(rstd2[:, 0, :], b_var[:, 0:CW], EPS / 2, rstd2[:, 0, :], ALU.add, ALU.mult).then_inc(refine_step[2], 1)
                dve.wait_ge(refine_step[2], 2 * c + 1)
                dve.scalar_tensor_tensor(rstd[:, 0, :], rstd2[:, 0, :], -1.5, rstd[:, 0, :], ALU.add, ALU.mult).then_inc(refine_step[2], 1)
                dve.wait_ge(refine_step[2], 2 * c + 2)
                dve.tensor_tensor(x2flat[:, bass.ds(c * CW, CW)], b_cen[:, 0:CW], rstd[:, 0, :], ALU.mult).then_inc(norm_ready[2], 1)

            start(stages, attend=lambda n: attend(n, n))
            for n in range(2, FIRST):
                attend(n, n)
            with dve.Fori(0, LOOPS) as r:
                for u in range(TILES):
                    if u == 2:
                        residual(r)
                    attend(TILES * r + (FIRST + u), FIRST + u)
                    if u == 3:
                        norm_out(r)

            def choose(c):
                if c == 0:
                    dve.wait_ge(pads_ready, 4)
                dve.wait_ge(logits_ready, c + 1)
                for t in range(TILES):
                    last = dve.max(top8[:, c, t, :], logits[:, c, t, 0:E])
                last.then_inc(top8_ready, 1)
                dve.wait_ge(top8_ready, c + 1)
                dve.tensor_copy(top6[:, c, :, 0:TOPK], top8[:, c, :, 0:TOPK]).then_inc(top6_ready, 1)
                dve.wait_ge(top6_ready, c + 1)
                for t in range(TILES):
                    last = dve.match_replace(marked[:, c, t, :], top6[:, c, t, :], logits[:, c, t, :], -1.0e38)
                last.then_inc(marked_ready, 1)
                dve.wait_ge(marked_ready, c + 1)
                dve.tensor_tensor(gsel[:, c, :, 0:E], logits[:, c, :, 0:E], marked[:, c, :, 0:E], ALU.not_equal).then_inc(chosen_ready, 1)

            def gate_scale(c):
                dve.wait_ge(lsel_ready, c + 1)
                dve.tensor_reduce(lsum[:, c, 0:2, :].rearrange("p a b -> p (a b)"),
                                  lboth[:, c, :, :, :].rearrange("p a b e -> p (a b) e"), AX_X, ALU.add).then_inc(lsum_step, 1)
                dve.wait_ge(lsum_step, 3 * c + 1)
                dve.scalar_tensor_tensor(lsum[:, c, 2, :], lsum[:, c, 0, :], 1e-9, lsum[:, c, 1, :], ALU.mult, ALU.add).then_inc(lsum_step, 1)
                dve.wait_ge(lsum_step, 3 * c + 2)
                dve.reciprocal(lsum[:, c, 3, :], lsum[:, c, 2, :]).then_inc(lsum_step, 1)

            def admit(c):
                dve.wait_ge(gT_mm, c + 1)
                if c:
                    dve.wait_ge(rank_ready, c)
                dve.tensor_tensor_scan(rank[:, c, :], ones_row[:, :], b_gT[c % 2][0:E, 0:CW], rank[:, c - 1, CW - 1:CW] if c else 0.0,
                                       ALU.mult, ALU.add).then_inc(rank_ready, 1)
                dve.wait_ge(rank_ready, c + 1)
                dve.wait_ge(gT_ready, c + 1)
                dve.scalar_tensor_tensor(gateT[:, c, :], rank[:, c, :], float(CAPACITY), gT[:, c, :], ALU.is_le, ALU.mult).then_inc(gateT_ready, 1)

            def times_up(k, c, first=False):
                dve.wait_ge(actg_ready, k + 1)
                if not first:
                    dve.wait_ge(hid_ready, k - 1)
                dve.tensor_tensor(prod[:, c % 2, :], b_gu[c % 2][1][:, 0:CW], act_g[:, c % 2, :], ALU.mult).then_inc(prod_ready, 1)

            def low(k, c, first=False):
                dve.wait_ge(hidh_ready, k + 1)
                if not first:
                    dve.wait_ge(down_mm, k + 1)
                dve.tensor_tensor(hidl[:, c, :], hid[:, c % 2, :], hidh[:, c, :].bitcast(F32), ALU.subtract).then_inc(hidl_ready, 1)

            def shared_hidden(c):
                times_up(c, c, c < 2)
                if c:
                    low(c - 1, c - 1, True)

            tail({"attend": lambda n: attend(n, n), "project": residual, "norm": norm_out, "choose": choose, "scale": gate_scale, "admit": admit,
                  "hidden": shared_hidden})

            def expert_turns(p):
                for c in range(CH):
                    times_up(CH * p + c, c)
                    low(CH * p + (c - 1), (c - 1) % CH)

            with dve.Fori(0, XP) as r:
                expert_turns(r + 1)
            low(CH * XP + CH - 1, CH - 1)
            for c in range(CH):
                dve.wait_ge(down_mm, CH * (XP + 1) + c + 1)
                dve.tensor_tensor(result[:, c, :], b_sum[c][:, 0:CW], h2[:, chunk[c]], ALU.add).then_inc(result_ready, 1)

        @block.gpsimd
        def _(pool):
            pool.memset(qdiag[:, :, :, :, :], 0.0).then_inc(pads_ready, 1)
            pool.memset(logits[:, :, :, E:E + 2], SENTINEL).then_inc(pads_ready, 1)
            pool.memset(top6[:, :, :, TOPK:8], SENTINEL).then_inc(pads_ready, 1)
            pool.memset(ones_row[:, :], 1.0).then_inc(pads_ready, 1)
            pool.memset(half[:, :], 1.0 / SHARED).then_inc(half_ready, 1)

            def square(n, c):
                pool.wait_ge(rstd_ready[n], c + 1)
                pool.tensor_tensor(rstd2[:, c, :], rstd[:, c, :], rstd[:, c, :], ALU.mult).then_inc(rstd2_ready[n], 1)

            stages = (None, None, None, None, lambda c: square(0, c), None, None, None, lambda c: square(1, c), None, None)

            def fetch_tokens(j, s, n):
                if n >= 2:
                    pool.wait_ge(v_mm, j - 1)
                pool.tensor_copy(xpair[:, s, :], xn[:, bass.ds(j * PW, PW)]).then_inc(xpair_ready, 1)

            def fetch_q(j, s, n):
                if n >= 2:
                    pool.wait_ge(scores_mm, j - 1)
                q = qflat[:, bass.ds(j * PW, PW)].rearrange("p (a b) -> p a b", a=2)
                pool.tensor_tensor(qdiag[:, s, :, :, 0:SEQ], bcast(q, 2, 2), bcast(bcast(c_(C_PARITY, 2), 1, 2), 3, SEQ),
                                   ALU.mult).then_inc(qdiag_ready, 1)

            def fetch_k(j, s, n):
                k = kflat[:, bass.ds(j * PW, PW)].rearrange("p (a b) -> p a b", a=2)
                pool.tensor_tensor(khead[:, s, :, :, :], bcast(k, 2, HP), bcast(bcast(c_(C_HP, HP), 1, 2), 3, SEQ),
                                   ALU.mult).then_inc(khead_ready, 1)

            def fetch(j, n):
                fetch_q(j, n % 2, n)
                fetch_k(j, n % 2, n)
                fetch_tokens(j, n % 2, n)

            def first_fetch(n):
                if n == 0:
                    pool.wait_ge(s_consts, 16)
                    pool.wait_ge(pads_ready, 1)
                    pool.wait_ge(q_ready, 1)
                    pool.wait_ge(k_ready, 1)
                fetch(n, n)

            start(stages, fetch=first_fetch)
            for n in range(2, TILES):
                fetch(n, n)
            pool.wait_ge(q_ready, CH)
            pool.wait_ge(k_ready, CH)
            for n in range(TILES, TILES + 3):
                fetch(n, n)

            def split_gate_up(p, hs, first=False):
                pool.wait_ge(wgu_high, p + 1)
                if not first:
                    pool.wait_ge(gu_mm, CH * (p - 1))
                pool.tensor_tensor(wl[:, hs, 0:2 * P], wraw[:, hs, 0:2 * P], wh[:, hs, 0:2 * P].bitcast(F32), ALU.subtract).then_inc(wgu_low, 1)

            def split_down(p, hs, first=False):
                pool.wait_ge(wd_high, p + 1)
                if not first:
                    pool.wait_ge(down_mm, CH * p)
                pool.tensor_tensor(wl[:, hs, 2 * P:], wraw[:, hs, 2 * P:], wh[:, hs, 2 * P:].bitcast(F32), ALU.subtract).then_inc(wd_low, 1)

            for p in range(2):
                split_gate_up(p, p, True)
                split_down(p, p, True)

            def lower_x(c):
                at = bass.ds(c * CW, CW)
                pool.wait_ge(x2h_ready, c + 1)
                pool.tensor_tensor(x2lflat[:, at], x2flat[:, at], x2hflat[:, at].bitcast(F32), ALU.subtract).then_inc(x2l_ready, 1)

            with pool.Fori(0, CH - 2) as r:
                for u in range(TILES):
                    fetch(TILES * r + (TILES + 3 + u), TILES + 3 + u)

            def chosen_exp(c):
                pool.wait_ge(logits_ready, c + 1)
                pool.wait_ge(top8_ready, c + 1)
                pool.tensor_tensor(lsel[:, c, :, :], logits[:, c, :, 0:E], bcast(top8[:, c, :, 0], 2, E), ALU.subtract).then_inc(lshift_ready, 1)
                pool.wait_ge(lexp_ready, c + 1)
                pool.wait_ge(chosen_ready, c + 1)
                pool.tensor_tensor(lsel[:, c, :, :], lexp[:, c, :, :], gsel[:, c, :, 0:E], ALU.mult).then_inc(lsel_ready, 1)

            def gates(c):
                pool.wait_ge(lsum_step, 3 * (c + 1))
                pool.tensor_tensor(gsel[:, c, :, E:2 * E], lsel[:, c, :, :], bcast(lsum[:, c, 3, :], 2, E), ALU.mult).then_inc(gsel_ready, 1)

            def gated(k, c, gate, first=False):
                pool.wait_ge(prod_ready, k + 1)
                if not first:
                    pool.wait_ge(hidl_ready, k - 1)
                pool.tensor_tensor(hid[:, c % 2, :], prod[:, c % 2, :], gate, ALU.mult).then_inc(hid_ready, 1)

            def expert_turns(p, gs, loads=0, first=False, last=False):
                if not first:
                    pool.wait_ge(s_gbc[gs], 16 * loads)
                for c in range(CH):
                    if first:
                        pool.wait_ge(s_gfirst[c], 2 * 16)
                    gated(CH * p + c, c, gbc[:, gs, chunk[c]])
                    if not last:
                        if c == 1:
                            split_gate_up(p + 1, gs % 2)
                        if c == 3:
                            split_down(p + 1, gs % 2)

            pool.wait_ge(half_ready, 1)
            tail({"fetch": lambda n: fetch(n, n), "upper": lower_x, "choose": chosen_exp, "scale": gates,
                  "hidden": lambda c: gated(c, c, half[:, :], c < 2)})
            for v in range(2):
                expert_turns(v + 1, v, first=True)
            with pool.Fori(0, XP // GS - 1) as r:
                for v in range(GS):
                    expert_turns(GS * r + (3 + v), (v + 2) % GS, r + 1)
            expert_turns(XP - 1, 2, XP // GS)
            expert_turns(XP, 3, XP // GS, last=True)


def _constants():
    c = np.zeros((P, CCOLS), np.float32)
    c[:, C_IDENT:C_IDENT + P] = np.eye(P)
    c[:, C_CENTER:C_CENTER + P] = 1.0 / P - np.eye(P)
    c[:, C_MEAN:C_MEAN + P] = 0.5 / P
    c[:, C_ONES:C_ONES + P] = 1.0
    tenth = np.float32(0.1)
    high = np.float32(np.round(float(tenth) * 2 ** 15) / 2 ** 15)
    eye = np.eye(SEQ, dtype=np.float32)
    idx = np.arange(SEQ)
    band = (np.abs(idx[:, None] - idx[None, :]) <= WINDOW).astype(np.float32)
    for r, part in enumerate((high, tenth - high)):
        for t in range(2):
            c[r * SEQ:(r + 1) * SEQ, C_BANDQ + t * QW:C_BANDQ + t * QW + SEQ] = eye * part
        c[r * SEQ:(r + 1) * SEQ, C_BANDK:C_BANDK + CW] = np.tile(band, (1, HEADS))
    for t in range(2):
        c[:, C_PARITY + t] = (np.arange(P) // HD) % 2 == t
        c[t * SEQ:(t + 1) * SEQ, C_IMAGE + t] = 1.0
    c[:, C_EPS] = EPS
    for hp in range(HP):
        c[:, C_HP + hp] = np.arange(P) // (2 * HD) == hp
    return c


def _rows(a):
    a = np.asarray(a)
    a = a.reshape(a.shape[0], -1)
    return np.concatenate([a, np.zeros((P - a.shape[0], a.shape[1]), a.dtype)]) if a.shape[0] < P else a


def kernel(**inputs):
    import concourse.bacc as _bacc
    from concourse.bass_utils import run_bass_kernel_spmd as _run

    f = {k: np.asarray(v) for k, v in inputs.items()}
    patches = f["x"].reshape(IMAGES, CHANNELS, GRID, PATCH, GRID, PATCH).transpose(1, 3, 5, 0, 2, 4).reshape(KT, P, N).transpose(1, 0, 2)
    w_patch = f["L0_tok_W_patch"].reshape(KT, P, P).transpose(1, 0, 2)
    wo = f["L0_attn_Wo"].T.reshape(HP, 2, HD, P).transpose(0, 2, 1, 3).reshape(HP * HD, 2 * P)
    blank = np.zeros_like(wo)
    wo = np.concatenate([np.concatenate([wo, blank], axis=1), np.concatenate([blank, wo], axis=1)])
    bv = f["L0_attn_bv"].reshape(HP, 2, HD).transpose(0, 2, 1).reshape(HP * HD, 2)
    spinor = f["L0_tok_W_spinor"]
    columns = [spinor, np.zeros((P, CO_AT - DS), spinor.dtype), f["L0_tok_W_coord"], f["L0_tok_W_out"],
               f["L0_attn_Wq"].T, f["L0_attn_Wk"].T, f["L0_attn_Wv"].T,
               wo, f["L0_ffn_router_w"].T, f["L0_tok_W_embed"], f["L0_tok_b_patch"], f["L0_tok_b_embed"], f["L0_tok_ln_gamma"],
               f["L0_tok_ln_beta"], f["L0_tok_b_out"], f["L0_attn_bq"], f["L0_attn_bk"], f["L0_attn_ocr_bias"], f["L0_attn_bo"],
               f["L0_tok_b_coord"], f["L0_tok_b_spinor"], bv, f["L0_tok_pos_embed"][0].T, f["L0_ffn_bias"][None, :]]
    weights = np.concatenate([_rows(a) for a in columns], axis=1)

    def up(shared, routed):
        both = np.concatenate([f[shared], f[routed]])
        return both.reshape(XP + 1, P, P).transpose(0, 2, 1)

    down = np.concatenate([f["L0_ffn_shared_w_down"], f["L0_ffn_w_down"]]).reshape(XP + 1, 2, P, FF).transpose(0, 1, 3, 2).reshape(XP + 1, P, P)
    experts = np.concatenate([up("L0_ffn_shared_w_gate", "L0_ffn_w_gate"), up("L0_ffn_shared_w_up", "L0_ffn_w_up"), down], axis=2)
    arrays = {"patches": patches, "w_patch": w_patch, "weights": weights, "consts": _constants(), "experts": experts}
    arrays = {k: np.ascontiguousarray(v) for k, v in arrays.items()}

    nc = _bacc.Bacc("TRN2", target_bir_lowering=False, num_devices=1)
    args = [nc.dram_tensor(k, v.shape, F32, kind="ExternalInput").ap() for k, v in arrays.items()]
    args.append(nc.dram_tensor("gate_scratch", (E, N), F32, kind="Internal").ap())
    args.append(nc.dram_tensor("out", (P, N), F32, kind="ExternalOutput").ap())
    build(nc, *args)
    r = _run(nc, [arrays], core_ids=[0])
    return np.ascontiguousarray(np.asarray(r.results[0]["out"]).T).reshape(IMAGES, SEQ, P)
```
